# Optimizing a Trainium2 kernel written in Bass

```python
import numpy as np
import jax
import jax.numpy as jnp

def _softmax(x, axis=-1):
    return jax.nn.softmax(x, axis=axis)

def _gelu(x):
    return jax.nn.gelu(x, approximate=True)

def _silu(x):
    return jax.nn.silu(x)

def _sigmoid(x):
    return jax.nn.sigmoid(x)

def _layernorm(x, axis=-1, eps=1e-05):
    m = jnp.mean(x, axis=axis, keepdims=True)
    v = jnp.var(x, axis=axis, keepdims=True)
    return (x - m) / jnp.sqrt(v + eps)

def _scatter_add(tgt, idx, src, axis=0):
    return tgt.at[idx].add(src)

def _segment_sum(src, seg, n):
    return jax.ops.segment_sum(src, seg, n)
kernel_name = 'mk_xattn_ffn_d1_seqx_r4_f50d2b'

def setup_inputs(seed: int=0):
    np.random.seed(seed)
    _w = jnp.asarray

    def _rec_inputs():
        import jax
        import jax.numpy as jnp
        _rk = jax.random.key(seed)
        x = -0.0002928 + 1 * jax.random.normal(jax.random.fold_in(_rk, 1), (8, 256, 512), jnp.float32)
        _lenS = 256 - jax.random.randint(jax.random.fold_in(_rk, 7), (8,), 0, max(1, 256 // 4) + 1, jnp.int32)
        _lenS2 = 256 - jax.random.randint(jax.random.fold_in(_rk, 8), (8,), 0, max(1, 256 // 4) + 1, jnp.int32)
        _ctx_2048P = jax.random.normal(jax.random.fold_in(_rk, 11), (8, 16, 512), jnp.float32)
        _ctx_2048c = jax.random.dirichlet(jax.random.fold_in(_rk, 511), 0.3 * jnp.ones((16,), jnp.float32), (8, 256))
        _ctx_2048t = jnp.einsum('bsk,bkd->bsd', _ctx_2048c, _ctx_2048P)
        _ctx_2048t = _ctx_2048t * jax.lax.rsqrt(jnp.mean(jnp.square(_ctx_2048t)) + 1e-12) * 0.953939
        ctx_2048 = -1.39393e-06 + 0.999914 * (_ctx_2048t + 0.3 * jax.random.normal(jax.random.fold_in(_rk, 611), (8, 256, 512), jnp.float32))
        _validS = jnp.arange(256)[None, :] < _lenS[:, None]
        _validS2 = jnp.arange(256)[None, :] < _lenS2[:, None]
        _causal = jnp.tril(jnp.ones((256, 256), dtype=bool))
        mask_Bx1x2048_fk1 = jnp.where(jnp.ones((8, 1, 512), dtype=bool), 1.0, 0.0).astype(jnp.float32)
        return (x, ctx_2048, mask_Bx1x2048_fk1)
    x, ctx_2048, mask_Bx1x2048_fk1 = _rec_inputs()

    def _L0_xattn_setup():
        import math
        import jax, jax.numpy as jnp
        import numpy as np
        SIZE = 256
        HEADS = 16
        HEAD_DIM = SIZE // HEADS
        B, T, S = (2, 512, 512)
        NEG = 1000000.0
        key = jax.random.key(seed)
        ks = jax.random.split(key, 10)
        target = jax.random.normal(ks[0], (B, SIZE, T), dtype=jnp.float32)
        source = jax.random.normal(ks[1], (B, SIZE, S), dtype=jnp.float32)
        target_mask = (jax.random.uniform(ks[2], (B, 1, T)) > 0.1).astype(jnp.float32)
        source_mask = (jax.random.uniform(ks[3], (B, 1, S)) > 0.1).astype(jnp.float32)
        scale = 1.0 / math.sqrt(SIZE)
        Wq = jax.random.normal(ks[4], (SIZE, SIZE), dtype=jnp.float32) * scale
        Wk = jax.random.normal(ks[5], (SIZE, SIZE), dtype=jnp.float32) * scale
        Wv = jax.random.normal(ks[6], (SIZE, SIZE), dtype=jnp.float32) * scale
        bq = jax.random.normal(ks[7], (SIZE,), dtype=jnp.float32) * 0.01
        bk = jax.random.normal(ks[8], (SIZE,), dtype=jnp.float32) * 0.01
        bv = jax.random.normal(ks[9], (SIZE,), dtype=jnp.float32) * 0.01
        return {'target': target, 'source': source, 'target_mask': target_mask, 'source_mask': source_mask, 'Wq': Wq, 'bq': bq, 'Wk': Wk, 'bk': bk, 'Wv': Wv, 'bv': bv}
    _L0_xattn_all = _L0_xattn_setup()
    _L0_xattn_in = {k: v for k, v in _L0_xattn_all.items() if k in ('Wq', 'bq', 'Wk', 'bk', 'Wv', 'bv')}
    del _L0_xattn_all

    def _L0_ffn_setup():
        import jax, jax.numpy as jnp
        import numpy as np
        TOP_K = 2
        key = jax.random.key(seed)
        k1, k2, k3, k4 = jax.random.split(key, 4)
        B, S, H, I, E = (2, 256, 512, 352, 8)
        hidden_states = jax.random.normal(k1, (B, S, H), dtype=jnp.float32)
        gate_w = jax.random.normal(k2, (E, H), dtype=jnp.float32) * (1.0 / np.sqrt(H))
        w1 = jax.random.normal(k3, (E, 2 * I, H), dtype=jnp.float32) * (1.0 / np.sqrt(H))
        w2 = jax.random.normal(k4, (E, H, I), dtype=jnp.float32) * (1.0 / np.sqrt(I))
        return {'hidden_states': hidden_states, 'gate_w': gate_w, 'w1': w1, 'w2': w2}
    _L0_ffn_all = _L0_ffn_setup()
    _L0_ffn_in = {k: v for k, v in _L0_ffn_all.items() if k in ('gate_w', 'w1', 'w2')}
    del _L0_ffn_all
    return {'x': x, 'ctx_2048': ctx_2048, 'mask_Bx1x2048_fk1': mask_Bx1x2048_fk1, 'L0_xattn_Wq': _L0_xattn_in['Wq'], 'L0_xattn_bq': _L0_xattn_in['bq'], 'L0_xattn_Wk': _L0_xattn_in['Wk'], 'L0_xattn_bk': _L0_xattn_in['bk'], 'L0_xattn_Wv': _L0_xattn_in['Wv'], 'L0_xattn_bv': _L0_xattn_in['bv'], 'L0_ffn_gate_w': _L0_ffn_in['gate_w'], 'L0_ffn_w1': _L0_ffn_in['w1'], 'L0_ffn_w2': _L0_ffn_in['w2']}

def reference(x, ctx_2048, mask_Bx1x2048_fk1, L0_xattn_Wq, L0_xattn_bq, L0_xattn_Wk, L0_xattn_bk, L0_xattn_Wv, L0_xattn_bv, L0_ffn_gate_w, L0_ffn_w1, L0_ffn_w2):
    import jax
    import jax.numpy as jnp

    def _L0_xattn_ref(target, source, target_mask, source_mask, Wq, bq, Wk, bk, Wv, bv):
        import math
        import jax, jax.numpy as jnp
        import numpy as np
        SIZE = 256
        HEADS = 16
        HEAD_DIM = SIZE // HEADS
        B, T, S = (2, 512, 512)
        NEG = 1000000.0
        b, _, t = target.shape
        s = source.shape[-1]
        q = jnp.einsum('oc,bct->bot', Wq, target) + bq[None, :, None]
        k = jnp.einsum('oc,bcs->bos', Wk, source) + bk[None, :, None]
        v = jnp.einsum('oc,bcs->bos', Wv, source) + bv[None, :, None]
        q = q.reshape(b, HEADS, HEAD_DIM, t)
        k = k.reshape(b, HEADS, HEAD_DIM, s)
        v = v.reshape(b, HEADS, HEAD_DIM, s)
        dot = jnp.einsum('bhdt,bhds->bhts', q, k) / math.sqrt(HEAD_DIM)
        mask = target_mask[:, :, :, None] * source_mask[:, :, None, :]
        dot = mask * dot - (1.0 - mask) * NEG
        amap = jax.nn.softmax(dot, axis=-1) * mask
        out = jnp.einsum('bhts,bhds->bhdt', amap, v)
        return out.reshape(b, HEADS * HEAD_DIM, t)

    def _L0_ffn_ref(hidden_states, gate_w, w1, w2):
        import jax, jax.numpy as jnp
        import numpy as np
        TOP_K = 2
        B, S, H = hidden_states.shape
        E = gate_w.shape[0]
        T = B * S
        x = hidden_states.reshape(T, H)
        logits = jnp.einsum('th,eh->te', x, gate_w)
        probs = jax.nn.softmax(logits, axis=-1)
        topw, sel = jax.lax.top_k(probs, TOP_K)
        topw = topw / jnp.sum(topw, axis=-1, keepdims=True)
        combine = jnp.zeros((T, E), dtype=x.dtype).at[jnp.arange(T)[:, None], sel].add(topw)
        gate_up = jnp.einsum('th,eoh->eto', x, w1)
        g, u = jnp.split(gate_up, 2, axis=-1)
        act = jax.nn.silu(g) * u
        expert_out = jnp.einsum('eti,ehi->eth', act, w2)
        out = jnp.einsum('eth,te->th', expert_out, combine)
        return out.reshape(B, S, H)
    x = x + _L0_xattn_ref(_layernorm(x, axis=-1), ctx_2048, mask_Bx1x2048_fk1, mask_Bx1x2048_fk1, L0_xattn_Wq, L0_xattn_bq, L0_xattn_Wk, L0_xattn_bk, L0_xattn_Wv, L0_xattn_bv)
    x = x + _L0_ffn_ref(_layernorm(x, axis=-1), L0_ffn_gate_w, L0_ffn_w1, L0_ffn_w2)
    return x

_drawn_inputs = setup_inputs


def setup_inputs(seed=0):
    import zlib

    import numpy as np

    out = dict(_drawn_inputs(seed))
    spreads = {}
    factors = {'L0_xattn_bq': 8.0, 'L0_xattn_bk': 8.0, 'L0_xattn_bv': 6.258}
    for name, (base, spread) in spreads.items():
        noise = np.random.default_rng([zlib.crc32(name.encode()), seed]).standard_normal(out[name].shape)
        drawn = base * np.exp(spread * noise) if base else spread * noise
        out[name] = jnp.asarray(drawn.astype(out[name].dtype))
    for name, factor in factors.items():
        out[name] = (out[name] * factor).astype(out[name].dtype)
    return out
```

```python
from contextlib import ExitStack

import numpy as np

import concourse.bass as bass
from concourse import mybir

F32 = mybir.dt.float32
BF16 = mybir.dt.bfloat16
U32 = mybir.dt.uint32
I32 = mybir.dt.int32
ALU = mybir.AluOpType
ACT = mybir.ActivationFunctionType
X = mybir.AxisListType.X

B, C, T = 8, 256, 512
H, D = 16, 16
P = 128
UNITS = B * C // P
UH = P // D
NEG = 1.0e6
SCALE = 1.0 / float(np.sqrt(D))
EPS = 1e-5
E, I = 8, 352
TOKENS = B * C
CAP = TOKENS + P
ROW = T + 2
NT = 48

PAIRS = [(0, 0), (0, 1), (1, 0), (1, 1), (0, 2), (2, 0)]
BIAS_ROW = D * len(PAIRS)
MAX_ROW = BIAS_ROW + 1
RAW_ROWS = BIAS_ROW + 1
ALL_ROWS = MAX_ROW + 3
ICHUNKS = [(0, 128), (128, 128), (256, 96)]

FIRST, LAST = -3, UNITS + 1
BODY = 4
STEADY = (1, 3)


class U:

    def __init__(self, c, k):
        self.c, self.k = c, k
        self.half = k % 2
        self.batch = c * 2 + k // 2
        self.parity = k // 2

    def __add__(self, n):
        k = self.k + n
        return U(self.c + k // BODY, k % BODY)

    def __sub__(self, n):
        return self + (-n)

    def static(self):
        return isinstance(self.c, int)

    def has(self):
        return (not self.static()) or 0 <= BODY * self.c + self.k < UNITS

    def rows(self):
        return bass.ds(self.batch * C + self.half * P, P)


def unit_at(n):
    return U(n // BODY, n % BODY)


class Count:

    def __init__(self, sem, events, step=1):
        self.sem, self.step = sem, step
        self.names = {n: events(unit_at(n)) for n in range(FIRST, LAST + 1)}
        self.before = {n: sum(len(self.names[v]) for v in range(FIRST, n)) for n in self.names}
        self.base = BODY * STEADY[0]
        self.body = sum(len(self.names[self.base + k]) for k in range(BODY))

    def number(self, u, name):
        if u.static():
            n = BODY * u.c + u.k
            return self.before[n] + self.names[n].index(name) + 1
        n = self.base + u.k
        at = self.before[n] + self.names[n].index(name) + 1
        return u.c * self.body + (at - self.body * STEADY[0])

    def slot(self, u, name, ring):
        if u.static():
            return (self.number(u, name) - 1) % ring
        assert self.body % ring == 0
        return (self.number(U(STEADY[0], u.k), name) - 1) % ring

    def exists(self, u, name):
        n = BODY * u.c + u.k if u.static() else self.base + u.k
        return n in self.names and name in self.names[n]

    def at(self, u, name, back=0):
        if not self.exists(u, name):
            return None
        n = self.number(u, name)
        if u.static() and n <= back:
            return None
        return (n - back) * self.step

    def total(self):
        return self.step * sum(len(v) for v in self.names.values())


def iterations(eng, unit):
    for n in range(FIRST, BODY * STEADY[0]):
        unit(unit_at(n))
    with eng.Fori(*STEADY) as c:
        for k in range(BODY):
            unit(U(c, k))
    for n in range(BODY * STEADY[1], LAST + 1):
        unit(unit_at(n))


MAX_SHARE = [6, 6, 6, 6, 6, 2, 0, 0]
NSLOT = 3


def tile_events(u):
    ev, m = [], 0
    for s, n in enumerate(MAX_SHARE):
        if (u + 1).has():
            ev += [("max", m + j) for j in range(n)]
            m += n
        if s == 2 and (u - 2).has():
            ev.append("logits")
        if s == 4 and (u - 2).has():
            ev.append("ranks")
    if (u + 1).has():
        ev.append("maxT")
    if (u + 3).has():
        ev += ["q", "k"]
    if (u + 1).has():
        ev.append("v")
    if (u - 1).has():
        ev.append("xT")
    return ev


def step_events(u):
    return [(s, j) for s in range(8) for j in range(2)] if u.has() else []


def build(nc, x, ctxt, mask, maskc, wq, wk, wv, bq, bk, bv, gate, w1, w2, ident, ut, iotas, out):
    top = ExitStack()
    with top:
        def dram(name, shape, dt):
            return nc.dram_tensor(name, shape, dt, kind="Internal").ap()

        split_d = dram("split_d", [2, 2, 3, P, T], BF16)
        mrow_d = dram("mrow_d", [2, B, T], BF16)
        pv_d = dram("pv_d", [2, 2, 4, 32, T], F32)
        recip_d = dram("recip_d", [2, UH, T], F32)
        routed_d = dram("routed_d", [E * CAP + 4 * P, ROW], F32)

        keep = {}

        def ksb(name, shape, dt):
            keep[name] = top.enter_context(nc.sbuf_tensor(name, shape, dt))
            return keep[name]

        idf = ksb("idf", [P, P], F32)
        counts = ksb("counts", [P, E], F32)
        io = ksb("io", [P, 96], F32)
        attention(nc, dram, x, ctxt, mask, maskc, wq, wk, wv, bq, bk, bv, gate, ident, ut, iotas, out,
                  split_d, mrow_d, pv_d, recip_d, routed_d, idf, counts, io)
        experts(nc, w1, w2, out, routed_d, idf, counts, io)


def attention(nc, dram, x, ctxt, mask, maskc, wq, wk, wv, bq, bk, bv, gate, ident, ut, iotas, out,
              split_d, mrow_d, pv_d, recip_d, routed_d, idf, counts, io):
    st = ExitStack()
    with st:
        def sb(name, shape, dt=F32):
            return st.enter_context(nc.sbuf_tensor(name, shape, dt))

        def sem(name):
            return st.enter_context(nc.semaphore(name))

        idb = sb("idb", [P, P], BF16)
        upper = sb("upper", [P, P], BF16)
        ones = sb("ones", [P, P], BF16)
        wq_s = sb("wq_s", [P, 2, C])
        wk_s = sb("wk_s", [P, 2, C])
        wv_s = sb("wv_s", [P, 2, C])
        bqk = sb("bqk", [P, 2, 2])
        bv_s = sb("bv_s", [P, C])
        gate_s = sb("gate_s", [P, 4, E])
        mall = sb("mall", [B, T])
        mrow = sb("mrow", [B, 2, T], BF16)
        xin = sb("xin", [P, 2, 2, T])
        cin = sb("cin", [P, 2, 2, T])
        xh = sb("xh", [P, 2, 2, T])
        mb = sb("mb", [P, 2, T])
        mc = sb("mc", [P, 2, 4])
        ln = sb("ln", [P, 2, 16])
        qkf = sb("qkf", [P, 2, 2, T])
        rest = sb("rest", [P, 2, T])
        parts = sb("parts", [P, 2, 3, T], BF16)
        qs = [sb(f"qs{i}", [P, UH, T], BF16) for i in range(2)]
        ks = [sb(f"ks{i}", [P, UH, T], BF16) for i in range(2)]
        vp = [sb(f"vp{i}", [P, 4, UH, 32]) for i in range(2)]
        pr = [sb(f"pr{i}", [P, 4, T]) for i in range(2)]
        ov = sb("ov", [P, 2, T])
        mx = sb("mx", [P, 32])
        mxr = sb("mxr", [P, 2, 32])
        mxp = sb("mxp", [P, 3, 32], BF16)
        mxt = sb("mxt", [96, P], BF16)
        den = sb("den", [P, 32])
        mden = sb("mden", [P, 32])
        rec = sb("rec", [P, 2, 32])
        num = sb("num", [P, T])
        rb = sb("rb", [P, T])
        xr = sb("xr", [P, T])
        att = sb("att", [P, T])
        x1 = sb("x1", [P, 2, T])
        l2 = sb("l2", [P, 16])
        xa = sb("xa", [P, 2, 2, ROW])
        xt = sb("xt", [P, 4, P])
        lg = sb("lg", [P, E])
        v8 = sb("v8", [P, 8])
        i8 = sb("i8", [P, 8], U32)
        i8f = sb("i8f", [P, 8])
        sel = sb("sel", [P, 2, E])
        selb = sb("selb", [P, E], BF16)
        gap = sb("gap", [P, 1])
        ex = sb("ex", [P, 1])
        ex1 = sb("ex1", [P, 1])
        vt = sb("vt", [P, 4, P])
        utf = sb("utf", [P, P])
        tok = sb("tok", [P, 1])
        rk = sb("rk", [P, 2, E])
        junk = sb("junk", [P, 2, E])
        posf = sb("posf", [P, 2])
        pos = sb("pos", [P, 2, 2], U32)

        tiles = [st.enter_context(nc.psum_tensor(f"tile{i}", [P, T], F32)) for i in range(NSLOT)]
        sc = [st.enter_context(nc.psum_tensor(f"sc{i}", [P, 2, T], F32)) for i in range(2)]
        pvb = st.enter_context(nc.psum_tensor("pvb", [P, T], F32))

        const_loaded = sem("const_loaded")
        const_made = sem("const_made")
        mrow_kept = sem("mrow_kept")

        def has(n, names, half=None):
            def events(u):
                return list(names) if (u + n).has() and half in (None, u.half) else []
            return events

        passed = sem("passed")

        def apart(eng, u):
            if not u.static():
                eng.sem_inc(passed, 1)

        ready = Count(sem("tile_ready"), tile_events)
        drained = Count(sem("tile_drained"), tile_events)
        scored = Count(sem("scored"), step_events)
        exped = Count(sem("exped"), step_events)
        pved = Count(sem("pved"), has(0, range(8)))
        pv_out = Count(sem("pv_out"), has(0, range(2)))
        pv_kept = [Count(sem(f"pv_kept{g}"), has(0, ["g"]), 16) for g in range(2)]
        loaded = Count(sem("batch_loaded"), has(3, ["batch"], 1), 64)
        stats = Count(sem("stats"), has(3, ["s0", "a0", "s1", "a1"], 1))
        rstd = Count(sem("rstd"), has(3, [("eps", 0), ("pow", 0), ("eps", 1), ("pow", 1)], 1))
        normed = Count(sem("normed"), has(3, [0, 1], 1))
        split = Count(sem("split"), has(2, [(t, o) for t in range(2) for o in range(4)]))
        split_kept = Count(sem("split_kept"), has(2, ["split"]), 32)
        stacked = [Count(sem(f"stacked{g}"), has(2, ["g"]), 16 * (2 * len(PAIRS) + 2)) for g in range(2)]
        vmade = Count(sem("vmade"), has(1, ["v"]))
        maxsplit = Count(sem("maxsplit"), has(1, ["neg", "p0", "r1", "p1", "p2"]))
        maxrows = Count(sem("maxrows"), has(1, ["m"]), 48)
        den_in = Count(sem("den_in"), has(-1, ["d"]), 32)
        rec_made = Count(sem("rec_made"), has(-1, ["r", "m"]))
        rec_kept = Count(sem("rec_kept"), has(-1, ["k"]), 16)
        post_in = Count(sem("post_in"), has(-1, ["p"]), 32)
        rb_in = Count(sem("rb_in"), has(-1, ["rb"]), 16)
        post = Count(sem("post"), has(-1, ["mul", "x1"]))
        x1_kept = Count(sem("x1_kept"), has(-1, ["x"]), 16)
        stats2 = Count(sem("stats2"), has(-1, ["s", "a"]))
        rstd2 = Count(sem("rstd2"), has(-1, ["eps", "pow"]))
        normed2 = Count(sem("normed2"), has(-1, [0, 1]))
        choice = Count(sem("choice"), has(-2, ["v8", "i8", "i8f", "s0", "s1", "selb", "gap"]))
        gate_exp = Count(sem("gate_exp"), has(-2, ["e"]))
        weight = Count(sem("weight"), has(-2, ["ex1", "w0", "w1", "t0", "t1", "tok"]))
        place = Count(sem("place"), has(-2, ["rk1", "rk2", "p0", "p1", "pos"]))
        routed = Count(sem("routed"), has(-2, [0, 1]), 16)

        block = st.enter_context(nc.Block())
        const = ((idf[:, :], ident),
                 (wq_s[:, :, :], wq.rearrange("(c p) o -> p c o", p=P)),
                 (wk_s[:, :, :], wk.rearrange("(c p) o -> p c o", p=P)),
                 (wv_s[:, :, :], wv.rearrange("(c p) o -> p c o", p=P)),
                 (bqk[:, 0, :], bq),
                 (bqk[:, 1, :], bk),
                 (bv_s[:, :], bv.rearrange("(o c) -> o c", o=1).broadcast_to([P, C])),
                 (gate_s[:, :, :], gate.rearrange("(c p) e -> p c e", p=P)),
                 (utf[:, :], ut),
                 (io[:, :], iotas),
                 (mall[:, :], mask))
        CONST = 16 * len(const)
        MADE = 11

        @block.sync
        def _(sp):
            for dst, src in const:
                sp.dma_start(dst, src).then_inc(const_loaded, 16)
            sp.wait_ge(const_made, MADE)
            sp.dma_start(mrow_d.rearrange("w b t -> b w t"), mrow[:, :, :]).then_inc(mrow_kept, 16)
            sp.wait_ge(mrow_kept, 16)

            def load(u):
                w = u + 3
                rows = bass.ds(w.batch * C, C)
                if (due := normed.at(u - 4, 1)) is not None:
                    sp.wait_ge(normed.sem, due)
                    apart(sp, u)
                if (due := vmade.at(u - 1, "v")) is not None:
                    sp.wait_ge(vmade.sem, due)
                    apart(sp, u)
                one = bass.ds(w.batch, 1)
                for dst, src in ((xin[:, w.parity], x[rows, :].rearrange("(c p) t -> p c t", p=P)),
                                 (cin[:, w.parity], ctxt[rows, :].rearrange("(c p) t -> p c t", p=P)),
                                 (mb[:, w.parity, :], mask[one, :].broadcast_to([P, T])),
                                 (mc[:, w.parity, :], maskc[:, one, :])):
                    sp.dma_start(dst, src).then_inc(loaded.sem, 16)

            def stack(u, g):
                w = u + 2
                if (due := scored.at(u, (4 * g + 3, 1))) is not None:
                    sp.wait_ge(scored.sem, due)
                    apart(sp, u)
                if (due := ready.at(u, ("max", 16 * g))) is not None:
                    sp.wait_ge(ready.sem, due)
                    apart(sp, u)
                heads = slice(4 * g, 4 * g + 4)
                for side, buf in ((0, qs[w.half]), (1, ks[w.half])):
                    for i, pair in enumerate(PAIRS):
                        sp.dma_start(buf[D * i:D * i + D, heads, :],
                                     split_d[w.half, side, pair[side]]
                                     .rearrange("(h d) t -> d h t", d=D)[:, heads, :]
                                     ).then_inc(stacked[g].sem, 16)
                    sp.dma_start(buf[BIAS_ROW:BIAS_ROW + 1, heads, :],
                                 mrow_d[side:side + 1, bass.ds(w.batch, 1), :].broadcast_to([1, 4, T])
                                 ).then_inc(stacked[g].sem, 16)

            def unit(u):
                if (u + 3).has() and u.half == 1:
                    load(u)
                if (u - 1).has():
                    v = u - 1
                    product = pv_d[v.half].rearrange("g h r t -> (g h) r t")
                    for g in range(2):
                        if (due := pv_kept[g].at(v, "g")) is not None:
                            sp.wait_ge(pv_kept[g].sem, due)
                            apart(sp, u)
                    if (due := rec_made.at(u - 1, "m")) is not None:
                        sp.wait_ge(rec_made.sem, due)
                        apart(sp, u)
                    sp.dma_start(den[:, :], product[:, D, :].rearrange("h (j t) -> h j t", t=32)
                                 ).then_inc(den_in.sem, 16)
                    sp.dma_start(mden[:, :], mask[bass.ds(v.batch, 1), :]
                                 .rearrange("o (j t) -> o j t", t=32).broadcast_to([UH, D, 32])
                                 ).then_inc(den_in.sem, 16)
                    if (due := post.at(u - 1, "x1")) is not None:
                        sp.wait_ge(post.sem, due)
                        apart(sp, u)
                    sp.dma_start(num[:, :], product[:, 0:D, :]).then_inc(post_in.sem, 16)
                    sp.dma_start(xr[:, :], x[v.rows(), :]).then_inc(post_in.sem, 16)
                    if (due := rec_made.at(u, "m")) is not None:
                        sp.wait_ge(rec_made.sem, due)
                        apart(sp, u)
                    sp.dma_start(recip_d[v.half].rearrange("h (j t) -> (h j) t", t=32), rec[:, 1, :]
                                 ).then_inc(rec_kept.sem, 16)
                    if (due := rec_kept.at(u, "k")) is not None:
                        sp.wait_ge(rec_kept.sem, due)
                        apart(sp, u)
                    sp.dma_start(rb[:, :], recip_d[v.half].rearrange("h (o t) -> h o t", o=1)
                                 .broadcast_to([UH, D, T])).then_inc(rb_in.sem, 16)
                if (u + 2).has():
                    w = u + 2
                    for g in range(2):
                        if (due := stacked[g].at(u - 2, "g")) is not None:
                            sp.wait_ge(stacked[g].sem, due)
                            apart(sp, u)
                    for side in range(2):
                        if (due := split.at(u, (side, 3))) is not None:
                            sp.wait_ge(split.sem, due)
                            apart(sp, u)
                        sp.dma_start(split_d[w.half, side].rearrange("i p t -> p i t"),
                                     parts[:, side]).then_inc(split_kept.sem, 16)
                    if (due := split_kept.at(u, "split")) is not None:
                        sp.wait_ge(split_kept.sem, due)
                        apart(sp, u)
                    stack(u, 0)
                if (u + 1).has():
                    w = u + 1
                    if (due := drained.at(u, "maxT")) is not None:
                        sp.wait_ge(drained.sem, due)
                        apart(sp, u)
                    if (due := scored.at(u - 1, (7, 1))) is not None:
                        sp.wait_ge(scored.sem, due)
                        apart(sp, u)
                    for i in range(3):
                        sp.dma_start(qs[w.half][MAX_ROW + i:MAX_ROW + i + 1, :, :]
                                     .rearrange("o h (c t) -> o (h c) t", t=P),
                                     mxt[32 * i:32 * i + 32, :]).then_inc(maxrows.sem, 16)
                if (u + 2).has():
                    stack(u, 1)
                if (u - 1).has():
                    v = u - 1
                    if (due := post.at(u, "x1")) is not None:
                        sp.wait_ge(post.sem, due)
                        apart(sp, u)
                    if (due := x1_kept.at(u - 1, "x")) is not None:
                        sp.wait_ge(x1_kept.sem, due)
                        apart(sp, u)
                    sp.dma_start(out[v.rows(), :], x1[:, v.half, :]).then_inc(x1_kept.sem, 16)

            iterations(sp, unit)
            sp.wait_ge(x1_kept.sem, x1_kept.total())

        @block.gpsimd
        def _(pool):
            pool.wait_ge(const_loaded, CONST)

            def part(u, side):
                w = u + 2
                src = qkf[:, w.half, side, :]
                if (due := drained.at(u - 1, "qk"[side])) is not None:
                    pool.wait_ge(drained.sem, due)
                    apart(pool, u)
                if (due := split_kept.at(u - 1, "split")) is not None:
                    pool.wait_ge(split_kept.sem, due)
                    apart(pool, u)
                pool.tensor_scalar(parts[:, side, 0, :], src, 1.0, None, ALU.mult).then_inc(split.sem, 1)
                if (due := split.at(u, (side, 0))) is not None:
                    pool.wait_ge(split.sem, due)
                    apart(pool, u)
                pool.tensor_tensor(rest[:, side, :], src, parts[:, side, 0, :], ALU.subtract
                                   ).then_inc(split.sem, 1)
                if (due := split.at(u, (side, 1))) is not None:
                    pool.wait_ge(split.sem, due)
                    apart(pool, u)
                pool.tensor_scalar(parts[:, side, 1, :], rest[:, side, :], 1.0, None, ALU.mult
                                   ).then_inc(split.sem, 1)
                if (due := split.at(u, (side, 2))) is not None:
                    pool.wait_ge(split.sem, due)
                    apart(pool, u)
                pool.tensor_tensor(parts[:, side, 2, :], rest[:, side, :], parts[:, side, 1, :],
                                   ALU.subtract).then_inc(split.sem, 1)

            def unit(u):
                if (u + 2).has():
                    part(u, 0)
                    part(u, 1)
                if (u - 1).has():
                    v = u - 1
                    if (due := post_in.at(u, "p")) is not None:
                        pool.wait_ge(post_in.sem, due)
                        apart(pool, u)
                    if (due := rb_in.at(u, "rb")) is not None:
                        pool.wait_ge(rb_in.sem, due)
                        apart(pool, u)
                    pool.tensor_tensor(att[:, :], num[:, :], rb[:, :], ALU.mult).then_inc(post.sem, 1)
                    if (due := post.at(u, "mul")) is not None:
                        pool.wait_ge(post.sem, due)
                        apart(pool, u)
                    if (due := x1_kept.at(u - 2, "x")) is not None:
                        pool.wait_ge(x1_kept.sem, due)
                        apart(pool, u)
                    pool.tensor_tensor(x1[:, v.half, :], att[:, :], xr[:, :], ALU.add
                                       ).then_inc(post.sem, 1)
                if (u + 3).has() and u.half == 1:
                    w = u + 3
                    if (due := drained.at(u - 3, "q")) is not None:
                        pool.wait_ge(drained.sem, due)
                        apart(pool, u)
                    for c in range(2):
                        if (due := stats.at(u, f"a{c}")) is not None:
                            pool.wait_ge(stats.sem, due)
                            apart(pool, u)
                        pool.tensor_scalar(ln[:, c, 9:10], ln[:, c, 7:8], EPS, None, ALU.add
                                           ).then_inc(rstd.sem, 1)
                        if (due := rstd.at(u, ("eps", c))) is not None:
                            pool.wait_ge(rstd.sem, due)
                            apart(pool, u)
                        pool.tensor_tensor(ln[:, c, 8:9], ln[:, c, 9:10], io[:, 1:2], ALU.pow
                                           ).then_inc(rstd.sem, 1)
                        if (due := rstd.at(u, ("pow", c))) is not None:
                            pool.wait_ge(rstd.sem, due)
                            apart(pool, u)
                        pool.tensor_scalar(xh[:, w.parity, c, :], xin[:, w.parity, c, :],
                                           ln[:, c, 6:7], ln[:, c, 8:9], ALU.subtract, ALU.mult
                                           ).then_inc(normed.sem, 1)
                if (u - 2).has():
                    v = u - 2
                    if (due := place.at(u, "pos")) is not None:
                        pool.wait_ge(place.sem, due)
                        apart(pool, u)
                    if (due := weight.at(u, "t1")) is not None:
                        pool.wait_ge(weight.sem, due)
                        apart(pool, u)
                    if (due := normed2.at(u - 1, 1)) is not None:
                        pool.wait_ge(normed2.sem, due)
                        apart(pool, u)
                    if (due := routed.at(u - 1, 1)) is not None:
                        pool.wait_ge(routed.sem, due)
                        apart(pool, u)
                    for j in range(2):
                        pool.indirect_dma_start(
                            routed_d, bass.IndirectOffsetOnAxis(ap=pos[:, v.half, j:j + 1], axis=0),
                            xa[:, v.half, j, :], None).then_inc(routed.sem, 16)
                if (u - 1).has():
                    v = u - 1
                    if (due := stats2.at(u, "a")) is not None:
                        pool.wait_ge(stats2.sem, due)
                        apart(pool, u)
                    pool.tensor_scalar(l2[:, 9:10], l2[:, 7:8], EPS, None, ALU.add
                                       ).then_inc(rstd2.sem, 1)
                    if (due := rstd2.at(u, "eps")) is not None:
                        pool.wait_ge(rstd2.sem, due)
                        apart(pool, u)
                    pool.tensor_tensor(l2[:, 8:9], l2[:, 9:10], io[:, 1:2], ALU.pow
                                       ).then_inc(rstd2.sem, 1)
                    if (due := rstd2.at(u, "pow")) is not None:
                        pool.wait_ge(rstd2.sem, due)
                        apart(pool, u)
                    if (due := routed.at(u - 1, 1)) is not None:
                        pool.wait_ge(routed.sem, due)
                        apart(pool, u)
                    for j in range(2):
                        pool.tensor_scalar(xa[:, v.half, j, 0:T], x1[:, v.half, :], l2[:, 6:7],
                                           l2[:, 8:9], ALU.subtract, ALU.mult).then_inc(normed2.sem, 1)

            iterations(pool, unit)
            pool.wait_ge(routed.sem, routed.total())

        @block.scalar
        def _(act):
            def product_out(u, g):
                if (due := pved.at(u, 4 * g + 3)) is not None:
                    act.wait_ge(pved.sem, due)
                if (due := pv_kept[g].at(u - 1, "g")) is not None:
                    act.wait_ge(pv_kept[g].sem, due)
                nc.scalar.activation(ov[:, g, :], pvb[:, :], ACT.Copy).then_inc(pv_out.sem, 1)
                if (due := pv_out.at(u, g)) is not None:
                    act.wait_ge(pv_out.sem, due)
                if (due := den_in.at(u - 1, "d")) is not None:
                    act.wait_ge(den_in.sem, due)
                if (due := post_in.at(u - 1, "p")) is not None:
                    act.wait_ge(post_in.sem, due)
                act.dma_start(pv_d[u.half, g].rearrange("h r t -> (h r) t"), ov[:, g, :]
                              ).then_inc(pv_kept[g].sem, 16)

            def unit(u):
                for s in range(8):
                    if u.has():
                        for j in range(2):
                            if (due := scored.at(u, (s, j))) is not None:
                                act.wait_ge(scored.sem, due)
                            if j == 0:
                                if (due := pved.at(u, s, back=2)) is not None:
                                    act.wait_ge(pved.sem, due)
                            nc.scalar.activation(pr[s % 2][:, 2 * j:2 * j + 2, :], sc[j][:, :, :],
                                                 ACT.Exp, scale=SCALE).then_inc(exped.sem, 1)
                        if s == 4:
                            product_out(u, 0)
                    if s == 3 and (u - 2).has():
                        if (due := choice.at(u, "gap")) is not None:
                            act.wait_ge(choice.sem, due)
                        if (due := weight.at(u - 1, "w1")) is not None:
                            act.wait_ge(weight.sem, due)
                        nc.scalar.activation(ex[:, :], gap[:, :], ACT.Exp).then_inc(gate_exp.sem, 1)
                if u.has():
                    product_out(u, 1)

            act.wait_ge(const_made, MADE)
            iterations(act, unit)
            for g in range(2):
                act.wait_ge(pv_kept[g].sem, pv_kept[g].total())

        @block.vector
        def _(dve):
            dve.wait_ge(const_loaded, CONST)
            dve.tensor_copy(idb[:, :], idf[:, :]).then_inc(const_made, 1)
            dve.tensor_copy(upper[:, :], utf[:, :]).then_inc(const_made, 1)
            dve.memset(ones[:, :], 1.0).then_inc(const_made, 1)
            for half in range(2):
                dve.memset(ks[half][96:128, :, :], 1.0).then_inc(const_made, 1)
                dve.memset(vp[half][:, :, :, D:], 1.0).then_inc(const_made, 1)
            dve.memset(counts[:, :], 0.0).then_inc(const_made, 1)
            dve.tensor_copy(tok[:, :], io[:, 0:1]).then_inc(const_made, 1)
            dve.tensor_copy(mrow[:, 0, :], mall[:, :]).then_inc(const_made, 1)
            dve.tensor_scalar(mrow[:, 1, :], mall[:, :], 1.0, NEG / SCALE, ALU.subtract, ALU.mult
                              ).then_inc(const_made, 1)
            dve.wait_ge(const_made, MADE)

            def norm_stats(u):
                w = u + 3
                if (due := loaded.at(u, "batch")) is not None:
                    dve.wait_ge(loaded.sem, due)
                if (due := normed.at(u - 2, 1)) is not None:
                    dve.wait_ge(normed.sem, due)
                for c in range(2):
                    dve.bn_stats(ln[:, c, 0:6], xin[:, w.parity, c, :]).then_inc(stats.sem, 1)
                    if (due := stats.at(u, f"s{c}")) is not None:
                        dve.wait_ge(stats.sem, due)
                        apart(dve, u)
                    dve.bn_aggr(ln[:, c, 6:8], ln[:, c, 0:6]).then_inc(stats.sem, 1)

            def norm2_stats(u):
                v = u - 1
                if (due := post.at(u, "x1")) is not None:
                    dve.wait_ge(post.sem, due)
                if (due := normed2.at(u - 1, 1)) is not None:
                    dve.wait_ge(normed2.sem, due)
                dve.bn_stats(l2[:, 0:6], x1[:, v.half, :]).then_inc(stats2.sem, 1)
                if (due := stats2.at(u, "s")) is not None:
                    dve.wait_ge(stats2.sem, due)
                    apart(dve, u)
                dve.bn_aggr(l2[:, 6:8], l2[:, 0:6]).then_inc(stats2.sem, 1)

            def reciprocals(u):
                if (due := den_in.at(u, "d")) is not None:
                    dve.wait_ge(den_in.sem, due)
                dve.reciprocal(rec[:, 0, :], den[:, :]).then_inc(rec_made.sem, 1)
                if (due := rec_made.at(u, "r")) is not None:
                    dve.wait_ge(rec_made.sem, due)
                if (due := rec_kept.at(u - 1, "k")) is not None:
                    dve.wait_ge(rec_kept.sem, due)
                dve.tensor_tensor(rec[:, 1, :], rec[:, 0, :], mden[:, :], ALU.mult
                                  ).then_inc(rec_made.sem, 1)

            def tile_of(u, name):
                if (due := ready.at(u, name)) is not None:
                    dve.wait_ge(ready.sem, due)
                return tiles[ready.slot(u, name, NSLOT)]

            def split_maxima(u):
                if (due := drained.at(u, ("max", 31))) is not None:
                    dve.wait_ge(drained.sem, due)
                dve.tensor_scalar(mxr[:, 0, :], mx[:, :], -1.0, None, ALU.mult).then_inc(maxsplit.sem, 1)
                dve.wait_ge(maxsplit.sem, maxsplit.at(u, "neg"))
                dve.tensor_copy(mxp[:, 0, :], mxr[:, 0, :]).then_inc(maxsplit.sem, 1)
                dve.wait_ge(maxsplit.sem, maxsplit.at(u, "p0"))
                dve.tensor_tensor(mxr[:, 1, :], mxr[:, 0, :], mxp[:, 0, :], ALU.subtract
                                  ).then_inc(maxsplit.sem, 1)
                dve.wait_ge(maxsplit.sem, maxsplit.at(u, "r1"))
                dve.tensor_copy(mxp[:, 1, :], mxr[:, 1, :]).then_inc(maxsplit.sem, 1)
                dve.wait_ge(maxsplit.sem, maxsplit.at(u, "p1"))
                dve.tensor_tensor(mxp[:, 2, :], mxr[:, 1, :], mxp[:, 1, :], ALU.subtract
                                  ).then_inc(maxsplit.sem, 1)

            def choose(u):
                dve.tensor_copy(lg[:, :], tile_of(u, "logits")[:, 0:E]).then_inc(drained.sem, 1)
                if (due := drained.at(u, "logits")) is not None:
                    dve.wait_ge(drained.sem, due)
                    apart(dve, u)
                dve.max(v8[:, :], lg[:, :]).then_inc(choice.sem, 1)
                if (due := choice.at(u, "v8")) is not None:
                    dve.wait_ge(choice.sem, due)
                    apart(dve, u)
                dve.max_index(i8[:, :], v8[:, :], lg[:, :]).then_inc(choice.sem, 1)
                if (due := choice.at(u, "i8")) is not None:
                    dve.wait_ge(choice.sem, due)
                dve.tensor_copy(i8f[:, :], i8[:, :]).then_inc(choice.sem, 1)
                if (due := choice.at(u, "i8f")) is not None:
                    dve.wait_ge(choice.sem, due)
                for j in range(2):
                    dve.tensor_scalar(sel[:, j, :], io[:, 8:16], i8f[:, j:j + 1], None, ALU.is_equal
                                      ).then_inc(choice.sem, 1)
                if (due := choice.at(u, "s1")) is not None:
                    dve.wait_ge(choice.sem, due)
                dve.tensor_tensor(selb[:, :], sel[:, 0, :], sel[:, 1, :], ALU.add).then_inc(choice.sem, 1)
                if (due := gate_exp.at(u - 1, "e")) is not None:
                    dve.wait_ge(gate_exp.sem, due)
                dve.tensor_tensor(gap[:, :], v8[:, 1:2], v8[:, 0:1], ALU.subtract).then_inc(choice.sem, 1)

            def weigh(u):
                v = u - 2
                if (due := gate_exp.at(u, "e")) is not None:
                    dve.wait_ge(gate_exp.sem, due)
                dve.tensor_scalar(ex1[:, :], ex[:, :], 1.0, None, ALU.add).then_inc(weight.sem, 1)
                if (due := weight.at(u, "ex1")) is not None:
                    dve.wait_ge(weight.sem, due)
                dve.reciprocal(xa[:, v.half, 0, T:T + 1], ex1[:, :]).then_inc(weight.sem, 1)
                if (due := weight.at(u, "w0")) is not None:
                    dve.wait_ge(weight.sem, due)
                dve.tensor_tensor(xa[:, v.half, 1, T:T + 1], xa[:, v.half, 0, T:T + 1], ex[:, :],
                                  ALU.mult).then_inc(weight.sem, 1)
                for j in range(2):
                    dve.tensor_copy(xa[:, v.half, j, T + 1:T + 2], tok[:, :]).then_inc(weight.sem, 1)
                if (due := weight.at(u, "t1")) is not None:
                    dve.wait_ge(weight.sem, due)
                dve.tensor_scalar(tok[:, :], tok[:, :], float(P), None, ALU.add).then_inc(weight.sem, 1)

            def rows_of(u):
                v = u - 2
                t = tile_of(u, "ranks")
                dve.tensor_tensor(rk[:, 0, :], t[:, 0:E], counts[:, :], ALU.add).then_inc(place.sem, 1)
                if (due := place.at(u, "rk1")) is not None:
                    dve.wait_ge(place.sem, due)
                dve.tensor_tensor(counts[:, :], t[:, E:2 * E], counts[:, :], ALU.add
                                  ).then_inc(drained.sem, 1)
                dve.tensor_tensor(rk[:, 1, :], rk[:, 0, :], io[:, 16:24], ALU.add).then_inc(place.sem, 1)
                if (due := place.at(u, "rk2")) is not None:
                    dve.wait_ge(place.sem, due)
                for j in range(2):
                    dve.scalar_tensor_tensor(out=junk[:, j, :], in0=sel[:, j, :], scalar=1.0,
                                             in1=rk[:, 1, :], op0=ALU.mult, op1=ALU.mult,
                                             accum_out=posf[:, j:j + 1]).then_inc(place.sem, 1)
                if (due := place.at(u, "p1")) is not None:
                    dve.wait_ge(place.sem, due)
                if (due := routed.at(u - 2, 1)) is not None:
                    dve.wait_ge(routed.sem, due)
                dve.tensor_copy(pos[:, v.half, :], posf[:, :]).then_inc(place.sem, 1)

            def unit(u):
                m = 0
                for s, n in enumerate(MAX_SHARE):
                    if (u + 1).has():
                        if m == 0:
                            if (due := maxsplit.at(u - 1, "neg")) is not None:
                                dve.wait_ge(maxsplit.sem, due)
                        for j in range(m, m + n):
                            t = tile_of(u, ("max", j))
                            dve.tensor_reduce(mx[:, j:j + 1], t[:, :], X, ALU.max).then_inc(drained.sem, 1)
                        m += n
                        if n and m == 32:
                            split_maxima(u)
                    if s == 0 and (u - 1).has():
                        reciprocals(u)
                    if s == 2 and (u - 2).has():
                        choose(u)
                    if s == 3 and (u + 3).has() and u.half == 1:
                        norm_stats(u)
                    if s == 4 and (u - 2).has():
                        rows_of(u)
                    if s == 5 and (u - 2).has():
                        weigh(u)
                    if s == 6 and (u - 1).has():
                        norm2_stats(u)
                if (u + 1).has():
                    t = tile_of(u, "maxT")
                    if (due := maxrows.at(u - 1, "m")) is not None:
                        dve.wait_ge(maxrows.sem, due)
                    dve.tensor_copy(mxt[:, :], t[:, :].bitcast(BF16)[0:96, 0:P]).then_inc(drained.sem, 1)
                if (u + 3).has():
                    w = u + 3
                    if (due := loaded.at(u if u.half == 1 else u - 1, "batch")) is not None:
                        dve.wait_ge(loaded.sem, due)
                    for side in range(2):
                        t = tile_of(u, "qk"[side])
                        if (due := split.at(u - 1, (side, 1))) is not None:
                            dve.wait_ge(split.sem, due)
                        dve.scalar_tensor_tensor(
                            out=qkf[:, w.half, side, :], in0=t[:, :],
                            scalar=bqk[:, side, w.half:w.half + 1], in1=mb[:, w.parity, :],
                            op0=ALU.add, op1=ALU.mult).then_inc(drained.sem, 1)
                if (u + 1).has():
                    w = u + 1
                    t = tile_of(u, "v")
                    dve.tensor_tensor(vt[:, :, :], t[:, :].rearrange("p (c o) -> p c o", c=4),
                                      bv_s[:, w.half * P:w.half * P + P].rearrange("p (a o) -> p a o", a=1)
                                      .broadcast_to([P, 4, P]), ALU.add).then_inc(drained.sem, 1)
                    if (due := drained.at(u, "v")) is not None:
                        dve.wait_ge(drained.sem, due)
                    if (due := pved.at(u - 1, 7)) is not None:
                        dve.wait_ge(pved.sem, due)
                    dve.tensor_tensor(vp[w.half][:, :, :, 0:D],
                                      vt[:, :, :].rearrange("p c (h d) -> p c h d", d=D),
                                      mc[:, w.parity, :].rearrange("p (c a b) -> p c a b", a=1, b=1)
                                      .broadcast_to([P, 4, UH, D]), ALU.mult).then_inc(vmade.sem, 1)
                if (u - 1).has():
                    dve.tensor_copy(xt[:, :, :], tile_of(u, "xT")[:, :].rearrange("p (c o) -> p c o", c=4)
                                    ).then_inc(drained.sem, 1)

            iterations(dve, unit)

        @block.tensor
        def _(pe):
            pe.wait_ge(const_made, MADE)

            def slot(u, name):
                if (due := drained.at(u, name, back=NSLOT)) is not None:
                    pe.wait_ge(drained.sem, due)
                return tiles[ready.slot(u, name, NSLOT)]

            def scores(u, s):
                g, c = s // 4, s % 4
                if s == 0:
                    if (due := maxrows.at(u - 1, "m")) is not None:
                        pe.wait_ge(maxrows.sem, due)
                for j in range(2):
                    if (due := exped.at(u, (s, j), back=2)) is not None:
                        pe.wait_ge(exped.sem, due)
                    for i in range(2):
                        h = 4 * g + 2 * j + i
                        last = nc.tensor.matmul(sc[j][:, i, :],
                                                ks[u.half][0:ALL_ROWS, h, c * P:c * P + P],
                                                qs[u.half][0:ALL_ROWS, h, :], start=True, stop=True)
                    last.then_inc(scored.sem, 1)

            def raw_scores(u, m):
                w, h, c = u + 1, m // 4, m % 4
                if m % 16 == 0:
                    if (due := stacked[m // 16].at(u - 1, "g")) is not None:
                        pe.wait_ge(stacked[m // 16].sem, due)
                t = slot(u, ("max", m))
                nc.tensor.matmul(t[:, :], qs[w.half][0:RAW_ROWS, h, c * P:c * P + P],
                                 ks[w.half][0:RAW_ROWS, h, :], start=True, stop=True
                                 ).then_inc(ready.sem, 1)

            def product(u, s):
                g, c = s // 4, s % 4
                if s == 0:
                    if (due := vmade.at(u - 1, "v")) is not None:
                        pe.wait_ge(vmade.sem, due)
                    if (due := pv_out.at(u - 1, 1)) is not None:
                        pe.wait_ge(pv_out.sem, due)
                if s == 4:
                    if (due := pv_out.at(u, 0)) is not None:
                        pe.wait_ge(pv_out.sem, due)
                if (due := exped.at(u, (s, 1))) is not None:
                    pe.wait_ge(exped.sem, due)
                for i in range(4):
                    last = nc.tensor.matmul(pvb[32 * i:32 * i + 32, :], vp[u.half][:, c, 4 * g + i, :],
                                            pr[s % 2][:, i, :], start=(c == 0), stop=(c == 3))
                last.then_inc(pved.sem, 1)

            def project(u):
                w = u + 3
                t = slot(u, "q")
                if (due := normed.at(u if u.half == 1 else u - 1, 1)) is not None:
                    pe.wait_ge(normed.sem, due)
                for c in range(2):
                    last = nc.tensor.matmul(t[:, :], wq_s[:, c, w.half * P:w.half * P + P],
                                            xh[:, w.parity, c, :], start=(c == 0), stop=(c == 1))
                last.then_inc(ready.sem, 1)
                t = slot(u, "k")
                if (due := loaded.at(u if u.half == 1 else u - 1, "batch")) is not None:
                    pe.wait_ge(loaded.sem, due)
                for c in range(2):
                    last = nc.tensor.matmul(t[:, :], wk_s[:, c, w.half * P:w.half * P + P],
                                            cin[:, w.parity, c, :], start=(c == 0), stop=(c == 1))
                last.then_inc(ready.sem, 1)

            def values(u):
                w = u + 1
                t = slot(u, "v")
                for s in range(4):
                    for c in range(2):
                        last = nc.tensor.matmul(t[:, s * P:s * P + P],
                                                cin[:, w.parity, c, s * P:s * P + P],
                                                wv_s[:, c, w.half * P:w.half * P + P],
                                                start=(c == 0), stop=(c == 1))
                last.then_inc(ready.sem, 1)

            def unit(u):
                m = 0
                for s, n in enumerate(MAX_SHARE):
                    if u.has():
                        scores(u, s)
                    if (u + 1).has():
                        for j in range(m, m + n):
                            raw_scores(u, j)
                        m += n
                    if s == 2 and (u - 2).has():
                        if (due := drained.at(u - 1, "xT")) is not None:
                            pe.wait_ge(drained.sem, due)
                        t = slot(u, "logits")
                        for c in range(4):
                            last = nc.tensor.matmul(t[:, 0:E], xt[:, c, :], gate_s[:, c, :],
                                                    start=(c == 0), stop=(c == 3))
                        last.then_inc(ready.sem, 1)
                    if s == 4 and (u - 2).has():
                        if (due := choice.at(u, "selb")) is not None:
                            pe.wait_ge(choice.sem, due)
                        t = slot(u, "ranks")
                        nc.tensor.matmul(t[:, 0:E], upper[:, :], selb[:, :], start=True, stop=True)
                        nc.tensor.matmul(t[:, E:2 * E], ones[:, :], selb[:, :], start=True, stop=True
                                         ).then_inc(ready.sem, 1)
                    if s == 7 and (u + 1).has():
                        if (due := maxsplit.at(u, "p2")) is not None:
                            pe.wait_ge(maxsplit.sem, due)
                        t = slot(u, "maxT")
                        nc.tensor.transpose(t[:, :].bitcast(BF16)[0:96, 0:P],
                                            mxp[:, :, :].rearrange("p i m -> p (i m)"), idb[:, :]
                                            ).then_inc(ready.sem, 1)
                    if u.has() and s:
                        product(u, s - 1)
                if u.has():
                    product(u, 7)
                if (u + 3).has():
                    project(u)
                if (u + 1).has():
                    values(u)
                if (u - 1).has():
                    v = u - 1
                    if (due := normed2.at(u, 0)) is not None:
                        pe.wait_ge(normed2.sem, due)
                    t = slot(u, "xT")
                    for c in range(4):
                        last = nc.tensor.transpose(t[:, c * P:c * P + P],
                                                   xa[:, v.half, 0, c * P:c * P + P], idf[:, :])
                    last.then_inc(ready.sem, 1)

            iterations(pe, unit)


def experts(nc, w1, w2, out, routed_d, idf, counts, io):
    G1, G2 = 4 * 2 * I, len(ICHUNKS) * T
    st = ExitStack()
    with st:
        def sb(name, shape, dt=F32):
            return st.enter_context(nc.sbuf_tensor(name, shape, dt))

        def sem(name):
            return st.enter_context(nc.semaphore(name))

        w1_s = sb("w1_s", [P, E * G1])
        w2_s = sb("w2_s", [P, E * G2])
        xl = sb("xl", [P, 2, ROW])
        xt = [sb(f"xtile{i}", [P, 4, P]) for i in range(2)]
        sg = sb("sg", [P, 2, I])
        ac = sb("ac", [P, 2, I])
        at = sb("at", [P, len(ICHUNKS), P])
        y = sb("y", [P, 2, T])
        meta = sb("meta", [P, 2, 2])
        metay = sb("metay", [P, 2, 1])
        ids = sb("ids", [P, 2, 1], U32)
        pad = sb("pad", [P, ROW])
        f = sb("f", [P, 12, E])
        fi = sb("fi", [P, 2, E], I32)
        padpos = sb("padpos", [P, E], U32)
        ge = sb("ge", [1, 3, NT * E])
        tf = sb("tf", [1, 5, NT])
        tab = sb("tab", [1, 4, NT], I32)
        pairf = sb("pairf", [1, 2])
        pairi = sb("pairi", [1, 4], I32)

        def pb(name):
            return st.enter_context(nc.psum_tensor(name, [P, T], F32))

        xtp, atp, dp = pb("xtp"), pb("atp"), pb("dp")
        gp = [pb(f"gp{i}") for i in range(2)]
        up = [pb(f"up{i}") for i in range(2)]

        passed = sem("passed")
        plan = sem("plan")
        planned = sem("planned")
        padded = sem("padded")
        weights_in = [sem(f"weights_in{e}") for e in range(E)]
        experts_in = sem("experts_in")
        xl_in = [sem(f"xl_in{k}") for k in range(2)]
        xt_ready, xt_made = sem("xt_ready"), sem("xt_made")
        copied = sem("copied")
        up_done, silu_done, act_done = sem("up_done"), sem("silu_done"), sem("act_done")
        at_ready, at_made = sem("at_ready"), sem("at_made")
        down_done, y_made, y_added, noted = sem("down_done"), sem("y_made"), sem("y_added"), sem("noted")
        block = st.enter_context(nc.Block())

        OFF1, OFF2, EXPERT, ROWS = range(4)

        def entry(eng, row, n, top):
            return eng.value_load(tab[0:1, row, bass.ds(n, 1)], min_val=0, max_val=top)

        def pairs(eng):
            eng.wait_ge(planned, 1)
            return eng.value_load(pairi[0:1, 1:2], min_val=TOKENS // P,
                                  max_val=(2 * TOKENS // P + E) // 2)

        def last_tile(eng):
            return eng.value_load(pairi[0:1, 3:4], min_val=2 * TOKENS // P - 1, max_val=NT - 1)

        def tiles(eng, tile, count):
            tile(0, 0)
            tile(1, 1)
            with eng.Fori(1, count) as i:
                tile(i * 2, 0)
                tile(i * 2 + 1, 1)

        def later(n, back):
            return not isinstance(n, int) or n >= back

        @block.sync
        def _(sp):
            for e in range(E):
                sp.dma_start(w1_s[:, e * G1:(e + 1) * G1].rearrange("p (c o) -> p c o", c=4),
                             w1[e].rearrange("(c p) o -> p c o", p=P)).then_inc(weights_in[e], 16)
                sp.dma_start(w2_s[:, e * G2:e * G2 + 2 * T].rearrange("p (c o) -> p c o", c=2),
                             w2[e, 0:2 * P, :].rearrange("(c p) o -> p c o", p=P)
                             ).then_inc(weights_in[e], 16)
                sp.dma_start(w2_s[0:I - 2 * P, e * G2 + 2 * T:(e + 1) * G2], w2[e, 2 * P:I, :]
                             ).then_inc(weights_in[e], 16)
            for e in range(E):
                sp.wait_ge(weights_in[e], 48)
                sp.sem_inc(experts_in, 1)

        @block.vector
        def _(dve):
            at_ = [0]

            def do(ins):
                at_[0] += 1
                ins.then_inc(plan, 1)
                dve.wait_ge(plan, at_[0])

            E8 = io[:, 8:16]
            NTF, CUM, SEG, T0, T1, PADP = range(6)
            do(dve.memset(pad[:, :], 0.0))
            do(dve.tensor_scalar(pad[:, T + 1:T + 2], io[:, 0:1], float(TOKENS), None, ALU.add))
            do(dve.tensor_tensor(f[:, T0, :], counts[:, :], io[:, 16:24], ALU.add))
            do(dve.tensor_scalar(f[:, PADP, :], f[:, T0, :], io[:, 0:1], None, ALU.add))
            do(dve.tensor_copy(padpos[:, :], f[:, PADP, :]))
            do(dve.tensor_scalar(f[:, T1, :], counts[:, :], float(P - 1), None, ALU.add))
            do(dve.tensor_copy(fi[:, 0, :], f[:, T1, :]))
            do(dve.tensor_scalar(fi[:, 1, :], fi[:, 0, :], 7, None, ALU.arith_shift_right))
            do(dve.tensor_copy(f[:, NTF, :], fi[:, 1, :]))
            do(dve.tensor_copy(f[:, CUM, 0:1], f[:, NTF, 0:1]))
            for e in range(1, E):
                do(dve.tensor_tensor(f[:, CUM, e:e + 1], f[:, CUM, e - 1:e], f[:, NTF, e:e + 1], ALU.add))
            do(dve.tensor_scalar(f[:, SEG, :], f[:, NTF, :], -float(P), float(CAP), ALU.mult, ALU.add))
            nt_e = [1, NT, E]
            num_n = io[0:1, 32:32 + NT].rearrange("p (n o) -> p n o", o=1).broadcast_to(nt_e)
            g0 = ge[:, 0, :].rearrange("p (n e) -> p n e", e=E)
            g1 = ge[:, 1, :].rearrange("p (n e) -> p n e", e=E)
            g2 = ge[:, 2, :].rearrange("p (n e) -> p n e", e=E)
            do(dve.tensor_copy(g2, num_n))
            do(dve.tensor_tensor(g0, g2, f[0:1, CUM:CUM + 1, :].broadcast_to(nt_e), ALU.is_ge))
            do(dve.tensor_tensor(g1, g0, f[0:1, SEG:SEG + 1, :].broadcast_to(nt_e), ALU.mult))
            do(dve.tensor_reduce(tf[:, 0, :], g0, X, ALU.add))
            do(dve.tensor_reduce(tf[:, 1, :], g1, X, ALU.add))
            do(dve.tensor_scalar(tf[:, 2, :], tf[:, 0, :], float(E - 1), None, ALU.min))
            do(dve.tensor_scalar(tab[:, OFF1, :], tf[:, 2, :], float(G1), None, ALU.mult))
            do(dve.tensor_scalar(tab[:, OFF2, :], tf[:, 2, :], float(G2), None, ALU.mult))
            do(dve.tensor_copy(tab[:, EXPERT, :], tf[:, 2, :]))
            do(dve.tensor_scalar(tf[:, 3, :], io[0:1, 32:32 + NT], float(P), None, ALU.mult))
            do(dve.tensor_tensor(tab[:, ROWS, :], tf[:, 3, :], tf[:, 1, :], ALU.add))
            do(dve.tensor_scalar(pairf[:, 0:1], f[0:1, CUM, E - 1:E], 1.0, None, ALU.add))
            do(dve.tensor_copy(pairi[:, 0:1], pairf[:, 0:1]))
            do(dve.tensor_scalar(pairi[:, 1:2], pairi[:, 0:1], 1, None, ALU.arith_shift_right))
            do(dve.tensor_scalar(pairi[:, 2:3], pairi[:, 1:2], 2.0, None, ALU.mult))
            do(dve.tensor_scalar(pairi[:, 3:4], pairi[:, 2:3], 1.0, None, ALU.subtract))
            dve.sem_inc(planned, 1)
            count = pairs(dve)

            def fetch(n, k):
                dve.wait_ge(xt_ready, n + 1)
                if later(n, 2):
                    dve.wait_ge(up_done, n - 1)
                dve.tensor_copy(xt[k][:, :, :], xtp[:, :].rearrange("p (c o) -> p c o", c=4)
                                ).then_inc(copied, 1)
                dve.tensor_copy(meta[:, k, :], xl[:, k, T:T + 2]).then_inc(xt_made, 1)

            def note(n, k):
                if later(n, 2):
                    dve.wait_ge(y_added, (n - 1) * 16)
                dve.wait_ge(xt_made, n + 1)
                dve.tensor_copy(metay[:, k, :], meta[:, k, 0:1]).then_inc(noted, 1)
                dve.tensor_copy(ids[:, k, :], meta[:, k, 1:2]).then_inc(noted, 1)

            def finish(n, k):
                dve.wait_ge(at_ready, n + 1)
                if later(n, 1):
                    dve.wait_ge(down_done, n)
                dve.tensor_copy(at[:, 0:2, :], atp[:, 0:2 * P].rearrange("p (c o) -> p c o", c=2)
                                ).then_inc(copied, 1)
                dve.tensor_copy(at[0:I - 2 * P, 2, :], atp[0:I - 2 * P, 2 * P:3 * P]
                                ).then_inc(at_made, 1)

            def scale(n, k):
                dve.wait_ge(down_done, n + 1)
                dve.wait_ge(noted, (n + 1) * 2)
                dve.tensor_scalar(y[:, k, :], dp[:, :], metay[:, k, 0:1], None, ALU.mult
                                  ).then_inc(y_made, 1)

            def tile(n, k):
                prev = not (isinstance(n, int) and n == 0)
                if prev:
                    finish(n - 1, 1 - k)
                fetch(n + 1, 1 - k)
                if prev:
                    scale(n - 1, 1 - k)
                note(n, k)
                dve.wait_ge(silu_done, n + 1)
                if later(n, 2):
                    dve.wait_ge(at_ready, n - 1)
                dve.tensor_tensor(ac[:, k, :], sg[:, k, :], up[k][:, 0:I], ALU.mult).then_inc(act_done, 1)

            fetch(0, 0)
            tiles(dve, tile, count)
            last = last_tile(dve)
            finish(last, 1)
            scale(last, 1)

        @block.scalar
        def _(act):
            count = pairs(act)
            act.wait_ge(padded, 16 * (E + 5))

            def load(n, k):
                if later(n, 2):
                    act.wait_ge(xt_made, n - 1)
                row = entry(act, ROWS, n, E * CAP + 3 * P)
                act.dma_start(xl[:, k, :], routed_d[bass.ds(row, P), :]).then_inc(xl_in[k], 16)

            def tile(n, k):
                load(n + 2, k)
                act.wait_ge(up_done, n + 1)
                if later(n, 2):
                    act.wait_ge(act_done, n - 1)
                nc.scalar.activation(sg[:, k, :], gp[k][:, 0:I], ACT.Silu).then_inc(silu_done, 1)

            load(0, 0)
            load(1, 1)
            tiles(act, tile, count)
            for k in range(2):
                act.wait_ge(xl_in[k], (count + 1) * 16)
            act.sem_inc(passed, 1)

        @block.gpsimd
        def _(pool):
            pool.wait_ge(plan, 5)
            for e in range(E):
                pool.indirect_dma_start(routed_d, bass.IndirectOffsetOnAxis(ap=padpos[:, e:e + 1], axis=0),
                                        pad[:, :], None).then_inc(padded, 16)
            for i in range(4):
                pool.dma_start(routed_d[E * CAP + i * P:E * CAP + (i + 1) * P, :], pad[:, :]
                               ).then_inc(padded, 16)
            pool.dma_start(out[TOKENS:TOKENS + P, :], pad[:, 0:T]).then_inc(padded, 16)
            pool.wait_ge(padded, 16 * (E + 5))
            count = pairs(pool)

            def tile(n, k):
                pool.wait_ge(y_made, n + 1)
                pool.wait_ge(noted, (n + 1) * 2)
                if later(n, 1):
                    pool.wait_ge(y_added, n * 16)
                pool.sem_inc(passed, 1)
                pool.indirect_dma_start(out, bass.IndirectOffsetOnAxis(ap=ids[:, k, :], axis=0),
                                        y[:, k, :], None, compute_op=ALU.add).then_inc(y_added, 16)

            tiles(pool, tile, count)
            pool.wait_ge(y_added, count * 32)

        @block.tensor
        def _(pe):
            count = pairs(pe)

            def transpose_rows(n, k):
                pe.wait_ge(xl_in[k], ((n - k) // 2 + 1) * 16)
                if later(n, 1):
                    pe.wait_ge(xt_made, n)
                for c in range(4):
                    last = nc.tensor.transpose(xtp[:, c * P:c * P + P], xl[:, k, c * P:c * P + P], idf[:, :])
                last.then_inc(xt_ready, 1)

            def gate_up(n, k):
                expert = entry(pe, EXPERT, n, E - 1)
                off = entry(pe, OFF1, n, (E - 1) * G1)
                pe.wait_ge(experts_in, expert + 1)
                pe.wait_ge(xt_made, n + 1)
                if later(n, 2):
                    pe.wait_ge(act_done, n - 1)
                for dst, o in ((gp[k], 0), (up[k], I)):
                    for c in range(4):
                        last = nc.tensor.matmul(dst[:, 0:I], xt[k][:, c, :],
                                                w1_s[:, bass.ds(off + (c * 2 * I + o), I)],
                                                start=(c == 0), stop=(c == 3))
                last.then_inc(up_done, 1)

            def transpose_act(n, k):
                pe.wait_ge(act_done, n + 1)
                if later(n, 1):
                    pe.wait_ge(at_made, n)
                for c, (o, w) in enumerate(ICHUNKS):
                    last = nc.tensor.transpose(atp[0:w, c * P:c * P + P], ac[:, k, o:o + w], idf[:, :])
                last.then_inc(at_ready, 1)

            def down(n, k):
                off = entry(pe, OFF2, n, (E - 1) * G2)
                pe.wait_ge(at_made, n + 1)
                if later(n, 1):
                    pe.wait_ge(y_made, n)
                for c, (o, w) in enumerate(ICHUNKS):
                    last = nc.tensor.matmul(dp[:, :], at[0:w, c, :], w2_s[0:w, bass.ds(off + c * T, T)],
                                            start=(c == 0), stop=(c == len(ICHUNKS) - 1))
                last.then_inc(down_done, 1)

            def tile(n, k):
                prev = not (isinstance(n, int) and n == 0)
                gate_up(n, k)
                if prev:
                    transpose_act(n - 1, 1 - k)
                transpose_rows(n + 1, 1 - k)
                if prev:
                    down(n - 1, 1 - k)

            transpose_rows(0, 0)
            tiles(pe, tile, count)
            last = last_tile(pe)
            transpose_act(last, 1)
            down(last, 1)


def kernel(**inputs):
    import concourse.bacc as bacc
    from concourse.bass_utils import run_bass_kernel_spmd

    def f32(name):
        return np.asarray(inputs[name])

    iotas = np.zeros((P, 96), np.float32)
    iotas[:, 0] = np.arange(P)
    iotas[:, 1] = -0.5
    iotas[:, 8:16] = np.arange(E)
    iotas[:, 16:24] = np.arange(E) * CAP
    iotas[:, 32:32 + NT] = np.arange(NT)
    arrays = {
        "x": f32("x").reshape(TOKENS, T),
        "ctxt": f32("ctx_2048").reshape(TOKENS, T),
        "mask": f32("mask_Bx1x2048_fk1").reshape(B, T),
        "wq": f32("L0_xattn_Wq").T, "wk": f32("L0_xattn_Wk").T, "wv": f32("L0_xattn_Wv").T,
        "maskc": f32("mask_Bx1x2048_fk1").reshape(B, 4, P).transpose(2, 0, 1),
        "bq": f32("L0_xattn_bq").reshape(2, P).T, "bk": f32("L0_xattn_bk").reshape(2, P).T, "bv": f32("L0_xattn_bv"),
        "gate": f32("L0_ffn_gate_w").T,
        "w1": f32("L0_ffn_w1").transpose(0, 2, 1), "w2": f32("L0_ffn_w2").transpose(0, 2, 1),
        "ident": np.eye(P, dtype=np.float32),
        "ut": np.triu(np.ones((P, P), np.float32), 1),
        "iotas": iotas,
    }
    arrays = {k: np.ascontiguousarray(v) for k, v in arrays.items()}
    nc = bacc.Bacc("TRN2", target_bir_lowering=False, num_devices=1)
    args = {k: nc.dram_tensor(k + "_dram", v.shape, mybir.dt.from_np(v.dtype), kind="ExternalInput").ap()
            for k, v in arrays.items()}
    out = nc.dram_tensor("out_dram", (TOKENS + P, T), F32, kind="ExternalOutput").ap()
    build(nc, out=out, **args)
    r = run_bass_kernel_spmd(nc, [{k + "_dram": v for k, v in arrays.items()}], core_ids=[0])
    return r.results[0]["out_dram"][:TOKENS].reshape(B, C, T)
```

```python
from contextlib import ExitStack

import numpy as np

import concourse.bass as bass
from concourse import mybir

F32 = mybir.dt.float32
BF16 = mybir.dt.bfloat16
U32 = mybir.dt.uint32
I32 = mybir.dt.int32
ALU = mybir.AluOpType
ACT = mybir.ActivationFunctionType
X = mybir.AxisListType.X

B, C, T = 8, 256, 512
H, D = 16, 16
P = 128
UNITS = B * C // P
UH = P // D
NEG = 1.0e6
SCALE = 1.0 / float(np.sqrt(D))
EPS = 1e-5
E, I = 8, 352
TOKENS = B * C
CAP = TOKENS + P
ROW = T + 2
NT = 48

PAIRS = [(0, 0), (0, 1), (0, 2), (1, 0), (1, 1), (2, 0)]
RUNS = [(0, 3, 0), (3, 2, 1), (5, 1, 2)]
BIAS_ROW = D * len(PAIRS)
MAX_ROW = BIAS_ROW + 1
RAW_ROWS = BIAS_ROW + 1
ALL_ROWS = MAX_ROW + 3
W1N, W2N = 4 * 2 * I, 3 * T
WN = W1N + W2N
OFFSET, EXPERT, ROWS = range(3)
WRING = 3
ICHUNKS = [(0, 128), (128, 128), (256, 96)]

FIRST, LAST = -3, UNITS + 1
BODY = 4
STEADY = (1, 3)


class U:

    def __init__(self, c, k):
        self.c, self.k = c, k
        self.half = k % 2
        self.batch = c * 2 + k // 2
        self.parity = k // 2

    def __add__(self, n):
        k = self.k + n
        return U(self.c + k // BODY, k % BODY)

    def __sub__(self, n):
        return self + (-n)

    def static(self):
        return isinstance(self.c, int)

    def has(self):
        return (not self.static()) or 0 <= BODY * self.c + self.k < UNITS

    def rows(self):
        return bass.ds(self.batch * C + self.half * P, P)


def unit_at(n):
    return U(n // BODY, n % BODY)


class Count:

    def __init__(self, sem, events, step=1):
        self.sem, self.step = sem, step
        self.names = {n: events(unit_at(n)) for n in range(FIRST, LAST + 1)}
        self.before = {n: sum(len(self.names[v]) for v in range(FIRST, n)) for n in self.names}
        self.base = BODY * STEADY[0]
        self.body = sum(len(self.names[self.base + k]) for k in range(BODY))

    def number(self, u, name):
        if u.static():
            n = BODY * u.c + u.k
            return self.before[n] + self.names[n].index(name) + 1
        n = self.base + u.k
        at = self.before[n] + self.names[n].index(name) + 1
        return u.c * self.body + (at - self.body * STEADY[0])

    def slot(self, u, name, ring):
        if u.static():
            return (self.number(u, name) - 1) % ring
        assert self.body % ring == 0
        return (self.number(U(STEADY[0], u.k), name) - 1) % ring

    def exists(self, u, name):
        n = BODY * u.c + u.k if u.static() else self.base + u.k
        return n in self.names and name in self.names[n]

    def at(self, u, name, back=0):
        if not self.exists(u, name):
            return None
        n = self.number(u, name)
        if u.static() and n <= back:
            return None
        return (n - back) * self.step

    def total(self):
        return self.step * sum(len(v) for v in self.names.values())


def iterations(eng, unit):
    for n in range(FIRST, BODY * STEADY[0]):
        unit(unit_at(n))
    with eng.Fori(*STEADY) as c:
        for k in range(BODY):
            unit(U(c, k))
    for n in range(BODY * STEADY[1], LAST + 1):
        unit(unit_at(n))


MAX_SHARE = [5, 5, 4, 5, 5, 5, 3, 0]
NSLOT = 3


def tile_events(u):
    ev, m = [], 0
    for s, n in enumerate(MAX_SHARE):
        if (u + 1).has():
            ev += [("max", m + j) for j in range(n)]
            m += n
        if s == 1 and (u - 2).has():
            ev.append("xT")
        if s == 3 and (u - 2).has():
            ev.append("logits")
        if s == 5 and (u - 2).has():
            ev.append("ranks")
        if s == 6 and (u + 3).has():
            ev.append("q")
        if s == 7:
            ev += ["maxT"] * (u + 1).has() + ["k"] * (u + 3).has()
    if (u + 1).has():
        ev.append("v")
    return ev


def step_events(u):
    return [(s, j) for s in range(8) for j in range(2)] if u.has() else []


def build(nc, x, ctxt, mask, maskc, wq, wk, wv, bq, bk, bv, gate, w1, w2, ident, ut, iotas, out):
    top = ExitStack()
    with top:
        def dram(name, shape, dt):
            return nc.dram_tensor(name, shape, dt, kind="Internal").ap()

        split_d = dram("split_d", [2, 2, 3, D, UH, T], BF16)
        mrow_d = dram("mrow_d", [2, B, T], BF16)
        pv_d = dram("pv_d", [2, 2, 4, 32, T], F32)
        recip_d = dram("recip_d", [2, UH, T], F32)
        routed_d = dram("routed_d", [E * CAP + 4 * P, ROW], F32)

        keep = {}

        def ksb(name, shape, dt):
            keep[name] = top.enter_context(nc.sbuf_tensor(name, shape, dt))
            return keep[name]

        idf = ksb("idf", [P, P], F32)
        counts = ksb("counts", [P, E], F32)
        io = ksb("io", [P, 96], F32)
        wring = ksb("wring", [P, WRING * WN], F32)
        tab = ksb("tab", [1, 3, NT], I32)
        ends = ksb("ends", [1, E], I32)
        pairi = ksb("pairi", [1, 4], I32)
        pad = ksb("pad", [P, ROW], F32)
        weights_in = [top.enter_context(nc.semaphore(f"weights_in{e}")) for e in range(E)]

        def load_expert(eng, e):
            at = (e % WRING) * WN
            eng.dma_start(wring[:, at:at + W1N].rearrange("p (c o) -> p c o", c=4),
                          w1[e].rearrange("(c p) o -> p c o", p=P)).then_inc(weights_in[e], 16)
            eng.dma_start(wring[:, at + W1N:at + W1N + 2 * T].rearrange("p (c o) -> p c o", c=2),
                          w2[e, 0:2 * P, :].rearrange("(c p) o -> p c o", p=P)
                          ).then_inc(weights_in[e], 16)
            eng.dma_start(wring[0:I - 2 * P, at + W1N + 2 * T:at + WN], w2[e, 2 * P:I, :]
                          ).then_inc(weights_in[e], 16)

        attention(nc, load_expert, x, ctxt, mask, maskc, wq, wk, wv, bq, bk, bv, gate, ident, ut, iotas, out,
                  split_d, mrow_d, pv_d, recip_d, routed_d, idf, counts, io, tab, ends, pairi, pad)
        experts(nc, load_expert, wring, weights_in, out, routed_d, idf, tab, ends, pairi)


def attention(nc, load_expert, x, ctxt, mask, maskc, wq, wk, wv, bq, bk, bv, gate, ident, ut, iotas, out,
              split_d, mrow_d, pv_d, recip_d, routed_d, idf, counts, io, tab, ends, pairi, pad):
    st = ExitStack()
    with st:
        def sb(name, shape, dt=F32):
            return st.enter_context(nc.sbuf_tensor(name, shape, dt))

        def sem(name):
            return st.enter_context(nc.semaphore(name))

        idb = sb("idb", [P, P], BF16)
        upper = sb("upper", [P, P], BF16)
        ones = sb("ones", [P, P], BF16)
        wq_s = sb("wq_s", [P, 2, C])
        wk_s = sb("wk_s", [P, 2, C])
        wv_s = sb("wv_s", [P, 2, C])
        bqk = sb("bqk", [P, 2, 2])
        bv_s = sb("bv_s", [P, C])
        gate_s = sb("gate_s", [P, 4, E])
        mall = sb("mall", [B, T])
        mrow = sb("mrow", [B, 2, T], BF16)
        xin = sb("xin", [P, 2, 2, T])
        cin = sb("cin", [P, 2, 2, T])
        xh = sb("xh", [P, 2, 2, T])
        mb = sb("mb", [P, 2, T])
        mc = sb("mc", [P, 2, 4])
        ln = sb("ln", [P, 2, 16])
        qkf = sb("qkf", [P, 2, 2, T])
        rest = sb("rest", [P, 2, T])
        parts = sb("parts", [P, 2, 3, T], BF16)
        qs = [sb(f"qs{i}", [P, UH, T], BF16) for i in range(2)]
        ks = [sb(f"ks{i}", [P, UH, T], BF16) for i in range(2)]
        vp = [sb(f"vp{i}", [P, 4, UH, 32]) for i in range(2)]
        pr = [sb(f"pr{i}", [P, 4, T]) for i in range(2)]
        ov = sb("ov", [P, 2, T])
        mx = sb("mx", [P, 32])
        mxr = sb("mxr", [P, 2, 32])
        mxp = sb("mxp", [P, 3, 32], BF16)
        mxt = sb("mxt", [96, P], BF16)
        den = sb("den", [P, 32])
        mden = sb("mden", [P, 32])
        rec = sb("rec", [P, 2, 32])
        num = sb("num", [P, T])
        rb = sb("rb", [P, T])
        xr = sb("xr", [P, T])
        att = sb("att", [P, T])
        x1 = sb("x1", [P, 2, T])
        l2 = sb("l2", [P, 16])
        xa = sb("xa", [P, 2, 2, ROW])
        xt = sb("xt", [P, 4, P])
        lg = sb("lg", [P, E])
        v8 = sb("v8", [P, 8])
        i8 = sb("i8", [P, 8], U32)
        i8f = sb("i8f", [P, 8])
        sel = sb("sel", [P, 2, E])
        selb = sb("selb", [P, E], BF16)
        gap = sb("gap", [P, 1])
        ex = sb("ex", [P, 1])
        ex1 = sb("ex1", [P, 1])
        vt = sb("vt", [P, 4, P])
        utf = sb("utf", [P, P])
        tok = sb("tok", [P, 1])
        rk = sb("rk", [P, 2, E])
        junk = sb("junk", [P, 2, E])
        f = sb("f", [P, 6, E])
        fi = sb("fi", [P, 2, E], I32)
        padrow = sb("padrow", [1, E], I32)
        ge = sb("ge", [1, 3, NT * E])
        tf = sb("tf", [1, 8, NT])
        pairf = sb("pairf", [1, 2])
        posf = sb("posf", [P, 2])
        pos = sb("pos", [P, 2, 2], U32)

        tiles = [st.enter_context(nc.psum_tensor(f"tile{i}", [P, T], F32)) for i in range(NSLOT)]
        sc = [st.enter_context(nc.psum_tensor(f"sc{i}", [P, 2, T], F32)) for i in range(2)]
        pvb = st.enter_context(nc.psum_tensor("pvb", [P, T], F32))

        const_loaded = sem("const_loaded")
        const_made = sem("const_made")
        mrow_kept = sem("mrow_kept")
        ones_made = sem("ones_made")
        plan = sem("plan")
        padded = sem("padded")

        def has(n, names, half=None):
            def events(u):
                return list(names) if (u + n).has() and half in (None, u.half) else []
            return events

        passed = sem("passed")

        def apart(eng, u):
            if not u.static():
                eng.sem_inc(passed, 1)

        ready = Count(sem("tile_ready"), tile_events)
        drained = Count(sem("tile_drained"), tile_events)
        scored = Count(sem("scored"), step_events)
        exped = Count(sem("exped"), step_events)
        pved = Count(sem("pved"), has(0, range(8)))
        pv_out = Count(sem("pv_out"), has(0, range(2)))
        pv_kept = [Count(sem(f"pv_kept{g}"), has(0, ["g"]), 16) for g in range(2)]
        loaded = Count(sem("batch_loaded"), has(3, ["batch"], 1), 64)
        stats = Count(sem("stats"), has(3, ["s0", "a0", "s1", "a1"], 1))
        rstd = Count(sem("rstd"), has(3, [("eps", 0), ("pow", 0), ("eps", 1), ("pow", 1)], 1))
        normed = Count(sem("normed"), has(3, [0, 1], 1))
        split = Count(sem("split"), has(2, [(t, o) for t in range(2) for o in range(4)]))
        split_kept = Count(sem("split_kept"), has(2, ["split"]), 6 * 16)
        stacked = [Count(sem(f"stacked{g}"), has(2, ["g"]), 16 * (2 * len(RUNS) + 2)) for g in range(2)]
        vmade = Count(sem("vmade"), has(1, ["v"]))
        maxsplit = Count(sem("maxsplit"), has(1, ["neg", "p0", "r1", "p1", "p2"]))
        maxrows = Count(sem("maxrows"), has(1, ["m"]), 48)
        den_in = Count(sem("den_in"), has(-1, ["d"]), 32)
        rec_made = Count(sem("rec_made"), has(-1, ["r", "m"]))
        rec_kept = Count(sem("rec_kept"), has(-1, ["k"]), 16)
        post_in = Count(sem("post_in"), has(-1, ["p"]), 32)
        rb_in = Count(sem("rb_in"), has(-1, ["rb"]), 16)
        post = Count(sem("post"), has(-1, ["mul", "x1"]))
        x1_kept = Count(sem("x1_kept"), has(-1, ["x"]), 16)
        stats2 = Count(sem("stats2"), has(-1, ["s", "a"]))
        rstd2 = Count(sem("rstd2"), has(-1, ["eps", "pow"]))
        normed2 = Count(sem("normed2"), has(-1, [0, 1]))
        choice = Count(sem("choice"), has(-2, ["v8", "i8", "i8f", "s0", "s1", "selb", "gap"]))
        gate_exp = Count(sem("gate_exp"), has(-2, ["e"]))
        weight = Count(sem("weight"), has(-2, ["ex1", "w0", "w1", "t0", "t1", "tok"]))
        place = Count(sem("place"), has(-2, ["rk1", "rk2", "p0", "p1", "pos"]))
        routed = Count(sem("routed"), has(-2, [0, 1]), 16)

        block = st.enter_context(nc.Block())
        const = ((idf[:, :], ident),
                 (wq_s[:, :, :], wq.rearrange("(c p) o -> p c o", p=P)),
                 (wk_s[:, :, :], wk.rearrange("(c p) o -> p c o", p=P)),
                 (wv_s[:, :, :], wv.rearrange("(c p) o -> p c o", p=P)),
                 (bqk[:, 0, :], bq),
                 (bqk[:, 1, :], bk),
                 (bv_s[:, :], bv.rearrange("(o c) -> o c", o=1).broadcast_to([P, C])),
                 (gate_s[:, :, :], gate.rearrange("(c p) e -> p c e", p=P)),
                 (utf[:, :], ut),
                 (io[:, :], iotas),
                 (mall[:, :], mask))
        CONST = 16 * len(const)
        MADE = 9

        @block.sync
        def _(sp):
            def load(u):
                w = u + 3
                rows = bass.ds(w.batch * C, C)
                if (due := normed.at(u - 4, 1)) is not None:
                    sp.wait_ge(normed.sem, due)
                    apart(sp, u)
                if (due := vmade.at(u - 1, "v")) is not None:
                    sp.wait_ge(vmade.sem, due)
                    apart(sp, u)
                one = bass.ds(w.batch, 1)
                for dst, src in ((xin[:, w.parity], x[rows, :].rearrange("(c p) t -> p c t", p=P)),
                                 (cin[:, w.parity], ctxt[rows, :].rearrange("(c p) t -> p c t", p=P)),
                                 (mb[:, w.parity, :], mask[one, :].broadcast_to([P, T])),
                                 (mc[:, w.parity, :], maskc[:, one, :])):
                    sp.dma_start(dst, src).then_inc(loaded.sem, 16)

            def stack(u, g):
                w = u + 2
                if (due := scored.at(u, (4 * g + 3, 1))) is not None:
                    sp.wait_ge(scored.sem, due)
                    apart(sp, u)
                if (due := ready.at(u, ("max", 16 * g))) is not None:
                    sp.wait_ge(ready.sem, due)
                    apart(sp, u)
                heads = slice(4 * g, 4 * g + 4)
                for side, buf in ((0, qs[w.half]), (1, ks[w.half])):
                    for first, n, part in RUNS:
                        if side == 0:
                            src = split_d[w.half, 0, part:part + 1, :, heads, :].broadcast_to([n, D, 4, T])
                        else:
                            src = split_d[w.half, 1, 0:n, :, heads, :]
                        sp.dma_start(buf[D * first:D * (first + n), heads, :],
                                     src.rearrange("i d h t -> i d (h t)")).then_inc(stacked[g].sem, 16)
                    sp.dma_start(buf[BIAS_ROW:BIAS_ROW + 1, heads, :],
                                 mrow_d[side:side + 1, bass.ds(w.batch, 1), :].broadcast_to([1, 4, T])
                                 ).then_inc(stacked[g].sem, 16)

            def unit(u):
                if (u + 3).has() and u.half == 1 and not (u.static() and BODY * u.c + u.k == FIRST):
                    load(u)
                if u.static() and 0 <= BODY * u.c + u.k < WRING:
                    load_expert(sp, BODY * u.c + u.k)
                if (u - 1).has():
                    v = u - 1
                    product = pv_d[v.half].rearrange("g h r t -> (g h) r t")
                    for g in range(2):
                        if (due := pv_kept[g].at(v, "g")) is not None:
                            sp.wait_ge(pv_kept[g].sem, due)
                            apart(sp, u)
                    if (due := rec_made.at(u - 1, "m")) is not None:
                        sp.wait_ge(rec_made.sem, due)
                        apart(sp, u)
                    sp.dma_start(den[:, :], product[:, D, :].rearrange("h (j t) -> h j t", t=32)
                                 ).then_inc(den_in.sem, 16)
                    sp.dma_start(mden[:, :], mask[bass.ds(v.batch, 1), :]
                                 .rearrange("o (j t) -> o j t", t=32).broadcast_to([UH, D, 32])
                                 ).then_inc(den_in.sem, 16)
                    if (due := post.at(u - 1, "x1")) is not None:
                        sp.wait_ge(post.sem, due)
                        apart(sp, u)
                    sp.dma_start(num[:, :], product[:, 0:D, :]).then_inc(post_in.sem, 16)
                    sp.dma_start(xr[:, :], x[v.rows(), :]).then_inc(post_in.sem, 16)
                    if (due := rec_made.at(u, "m")) is not None:
                        sp.wait_ge(rec_made.sem, due)
                        apart(sp, u)
                    sp.dma_start(recip_d[v.half].rearrange("h (j t) -> (h j) t", t=32), rec[:, 1, :]
                                 ).then_inc(rec_kept.sem, 16)
                    if (due := rec_kept.at(u, "k")) is not None:
                        sp.wait_ge(rec_kept.sem, due)
                        apart(sp, u)
                    sp.dma_start(rb[:, :], recip_d[v.half].rearrange("h (o t) -> h o t", o=1)
                                 .broadcast_to([UH, D, T])).then_inc(rb_in.sem, 16)
                if (u + 2).has():
                    w = u + 2
                    for g in range(2):
                        if (due := stacked[g].at(u - 2, "g")) is not None:
                            sp.wait_ge(stacked[g].sem, due)
                            apart(sp, u)
                    for side in range(2):
                        if (due := split.at(u, (side, 3))) is not None:
                            sp.wait_ge(split.sem, due)
                            apart(sp, u)
                        for i in range(3):
                            sp.dma_start(split_d[w.half, side, i].rearrange("d h t -> h d t"),
                                         parts[:, side, i, :]).then_inc(split_kept.sem, 16)
                    if (due := split_kept.at(u, "split")) is not None:
                        sp.wait_ge(split_kept.sem, due)
                        apart(sp, u)
                    stack(u, 0)
                if (u + 1).has():
                    w = u + 1
                    if (due := drained.at(u, "maxT")) is not None:
                        sp.wait_ge(drained.sem, due)
                        apart(sp, u)
                    if (due := scored.at(u - 1, (7, 1))) is not None:
                        sp.wait_ge(scored.sem, due)
                        apart(sp, u)
                    for i in range(3):
                        sp.dma_start(qs[w.half][MAX_ROW + i:MAX_ROW + i + 1, :, :]
                                     .rearrange("o h (c t) -> o (h c) t", t=P),
                                     mxt[32 * i:32 * i + 32, :]).then_inc(maxrows.sem, 16)
                if (u + 2).has():
                    stack(u, 1)
                if (u - 1).has():
                    v = u - 1
                    if (due := post.at(u, "x1")) is not None:
                        sp.wait_ge(post.sem, due)
                        apart(sp, u)
                    if (due := x1_kept.at(u - 1, "x")) is not None:
                        sp.wait_ge(x1_kept.sem, due)
                        apart(sp, u)
                    sp.dma_start(out[v.rows(), :], x1[:, v.half, :]).then_inc(x1_kept.sem, 16)

            for dst, src in const:
                sp.dma_start(dst, src).then_inc(const_loaded, 16)
            load(unit_at(FIRST))
            sp.wait_ge(const_made, MADE)
            sp.wait_ge(ones_made, 4)
            sp.dma_start(mrow_d.rearrange("w b t -> b w t"), mrow[:, :, :]).then_inc(mrow_kept, 16)
            sp.wait_ge(mrow_kept, 16)
            for i in range(4):
                sp.dma_start(routed_d[E * CAP + i * P:E * CAP + (i + 1) * P, :], pad[:, :]
                             ).then_inc(padded, 16)
            sp.dma_start(out[TOKENS:TOKENS + P, :], pad[:, 0:T]).then_inc(padded, 16)
            iterations(sp, unit)
            sp.wait_ge(plan, 2)
            for e in range(E):
                row = sp.value_load(padrow[0:1, e:e + 1], min_val=e * CAP, max_val=e * CAP + TOKENS)
                sp.dma_start(routed_d[bass.ds(row, P), :], pad[:, :]).then_inc(padded, 16)
            sp.wait_ge(padded, 16 * (E + 5))
            sp.wait_ge(x1_kept.sem, x1_kept.total())

        @block.gpsimd
        def _(pool):
            for half in range(2):
                pool.memset(ks[half][96:128, :, :], 1.0).then_inc(ones_made, 1)
                pool.wait_ge(ones_made, 2 * half + 1)
                pool.memset(vp[half][:, :, :, D:], 1.0).then_inc(ones_made, 1)
                pool.wait_ge(ones_made, 2 * half + 2)
            pool.wait_ge(const_loaded, CONST)

            def part(u, side):
                w = u + 2
                src = qkf[:, w.half, side, :]
                if (due := drained.at(u - 1, "qk"[side])) is not None:
                    pool.wait_ge(drained.sem, due)
                    apart(pool, u)
                if (due := split_kept.at(u - 1, "split")) is not None:
                    pool.wait_ge(split_kept.sem, due)
                    apart(pool, u)
                pool.tensor_scalar(parts[:, side, 0, :], src, 1.0, None, ALU.mult).then_inc(split.sem, 1)
                if (due := split.at(u, (side, 0))) is not None:
                    pool.wait_ge(split.sem, due)
                    apart(pool, u)
                pool.tensor_tensor(rest[:, side, :], src, parts[:, side, 0, :], ALU.subtract
                                   ).then_inc(split.sem, 1)
                if (due := split.at(u, (side, 1))) is not None:
                    pool.wait_ge(split.sem, due)
                    apart(pool, u)
                pool.tensor_scalar(parts[:, side, 1, :], rest[:, side, :], 1.0, None, ALU.mult
                                   ).then_inc(split.sem, 1)
                if (due := split.at(u, (side, 2))) is not None:
                    pool.wait_ge(split.sem, due)
                    apart(pool, u)
                pool.tensor_tensor(parts[:, side, 2, :], rest[:, side, :], parts[:, side, 1, :],
                                   ALU.subtract).then_inc(split.sem, 1)

            def unit(u):
                if (u + 2).has():
                    part(u, 0)
                    part(u, 1)
                if (u - 1).has():
                    v = u - 1
                    if (due := post_in.at(u, "p")) is not None:
                        pool.wait_ge(post_in.sem, due)
                        apart(pool, u)
                    if (due := rb_in.at(u, "rb")) is not None:
                        pool.wait_ge(rb_in.sem, due)
                        apart(pool, u)
                    pool.tensor_tensor(att[:, :], num[:, :], rb[:, :], ALU.mult).then_inc(post.sem, 1)
                    if (due := post.at(u, "mul")) is not None:
                        pool.wait_ge(post.sem, due)
                        apart(pool, u)
                    if (due := x1_kept.at(u - 2, "x")) is not None:
                        pool.wait_ge(x1_kept.sem, due)
                        apart(pool, u)
                    pool.tensor_tensor(x1[:, v.half, :], att[:, :], xr[:, :], ALU.add
                                       ).then_inc(post.sem, 1)
                if (u + 3).has() and u.half == 1:
                    w = u + 3
                    if (due := drained.at(u - 3, "q")) is not None:
                        pool.wait_ge(drained.sem, due)
                        apart(pool, u)
                    for c in range(2):
                        if (due := stats.at(u, f"a{c}")) is not None:
                            pool.wait_ge(stats.sem, due)
                            apart(pool, u)
                        pool.tensor_scalar(ln[:, c, 9:10], ln[:, c, 7:8], EPS, None, ALU.add
                                           ).then_inc(rstd.sem, 1)
                        if (due := rstd.at(u, ("eps", c))) is not None:
                            pool.wait_ge(rstd.sem, due)
                            apart(pool, u)
                        pool.tensor_tensor(ln[:, c, 8:9], ln[:, c, 9:10], io[:, 1:2], ALU.pow
                                           ).then_inc(rstd.sem, 1)
                        if (due := rstd.at(u, ("pow", c))) is not None:
                            pool.wait_ge(rstd.sem, due)
                            apart(pool, u)
                        pool.tensor_scalar(xh[:, w.parity, c, :], xin[:, w.parity, c, :],
                                           ln[:, c, 6:7], ln[:, c, 8:9], ALU.subtract, ALU.mult
                                           ).then_inc(normed.sem, 1)
                if (u - 2).has():
                    v = u - 2
                    if (due := place.at(u, "pos")) is not None:
                        pool.wait_ge(place.sem, due)
                        apart(pool, u)
                    if (due := weight.at(u, "t1")) is not None:
                        pool.wait_ge(weight.sem, due)
                        apart(pool, u)
                    if (due := normed2.at(u - 1, 1)) is not None:
                        pool.wait_ge(normed2.sem, due)
                        apart(pool, u)
                    if (due := routed.at(u - 1, 1)) is not None:
                        pool.wait_ge(routed.sem, due)
                        apart(pool, u)
                    for j in range(2):
                        pool.indirect_dma_start(
                            routed_d, bass.IndirectOffsetOnAxis(ap=pos[:, v.half, j:j + 1], axis=0),
                            xa[:, v.half, j, :], None).then_inc(routed.sem, 16)
                if (u - 1).has():
                    v = u - 1
                    if (due := stats2.at(u, "a")) is not None:
                        pool.wait_ge(stats2.sem, due)
                        apart(pool, u)
                    pool.tensor_scalar(l2[:, 9:10], l2[:, 7:8], EPS, None, ALU.add
                                       ).then_inc(rstd2.sem, 1)
                    if (due := rstd2.at(u, "eps")) is not None:
                        pool.wait_ge(rstd2.sem, due)
                        apart(pool, u)
                    pool.tensor_tensor(l2[:, 8:9], l2[:, 9:10], io[:, 1:2], ALU.pow
                                       ).then_inc(rstd2.sem, 1)
                    if (due := rstd2.at(u, "pow")) is not None:
                        pool.wait_ge(rstd2.sem, due)
                        apart(pool, u)
                    if (due := routed.at(u - 1, 1)) is not None:
                        pool.wait_ge(routed.sem, due)
                        apart(pool, u)
                    for j in range(2):
                        pool.tensor_scalar(xa[:, v.half, j, 0:T], x1[:, v.half, :], l2[:, 6:7],
                                           l2[:, 8:9], ALU.subtract, ALU.mult).then_inc(normed2.sem, 1)

            iterations(pool, unit)
            pool.wait_ge(routed.sem, routed.total())

        @block.scalar
        def _(act):
            def product_out(u, g):
                if (due := pved.at(u, 4 * g + 3)) is not None:
                    act.wait_ge(pved.sem, due)
                if (due := pv_kept[g].at(u - 1, "g")) is not None:
                    act.wait_ge(pv_kept[g].sem, due)
                nc.scalar.activation(ov[:, g, :], pvb[:, :], ACT.Copy).then_inc(pv_out.sem, 1)
                if (due := pv_out.at(u, g)) is not None:
                    act.wait_ge(pv_out.sem, due)
                if (due := den_in.at(u - 1, "d")) is not None:
                    act.wait_ge(den_in.sem, due)
                if (due := post_in.at(u - 1, "p")) is not None:
                    act.wait_ge(post_in.sem, due)
                act.dma_start(pv_d[u.half, g].rearrange("h r t -> (h r) t"), ov[:, g, :]
                              ).then_inc(pv_kept[g].sem, 16)

            def unit(u):
                for s in range(8):
                    if u.has():
                        for j in range(2):
                            if (due := scored.at(u, (s, j))) is not None:
                                act.wait_ge(scored.sem, due)
                            if j == 0:
                                if (due := pved.at(u, s, back=2)) is not None:
                                    act.wait_ge(pved.sem, due)
                            nc.scalar.activation(pr[s % 2][:, 2 * j:2 * j + 2, :], sc[j][:, :, :],
                                                 ACT.Exp, scale=SCALE).then_inc(exped.sem, 1)
                        if s == 4:
                            product_out(u, 0)
                    if s == 5 and (u - 2).has():
                        if (due := choice.at(u, "gap")) is not None:
                            act.wait_ge(choice.sem, due)
                        if (due := weight.at(u - 1, "w1")) is not None:
                            act.wait_ge(weight.sem, due)
                        nc.scalar.activation(ex[:, :], gap[:, :], ACT.Exp).then_inc(gate_exp.sem, 1)
                if u.has():
                    product_out(u, 1)

            act.wait_ge(const_made, MADE)
            iterations(act, unit)
            for g in range(2):
                act.wait_ge(pv_kept[g].sem, pv_kept[g].total())

        @block.vector
        def _(dve):
            dve.memset(pad[:, 0:T + 1], 0.0).then_inc(const_made, 1)
            dve.wait_ge(const_loaded, CONST)
            dve.tensor_scalar(pad[:, T + 1:T + 2], io[:, 0:1], float(TOKENS), None, ALU.add
                              ).then_inc(const_made, 1)
            dve.tensor_copy(idb[:, :], idf[:, :]).then_inc(const_made, 1)
            dve.tensor_copy(upper[:, :], utf[:, :]).then_inc(const_made, 1)
            dve.memset(ones[:, :], 1.0).then_inc(const_made, 1)
            dve.memset(counts[:, :], 0.0).then_inc(const_made, 1)
            dve.tensor_copy(tok[:, :], io[:, 0:1]).then_inc(const_made, 1)
            dve.tensor_copy(mrow[:, 0, :], mall[:, :]).then_inc(const_made, 1)
            dve.tensor_scalar(mrow[:, 1, :], mall[:, :], 1.0, NEG / SCALE, ALU.subtract, ALU.mult
                              ).then_inc(const_made, 1)
            dve.wait_ge(const_made, MADE)

            def norm_stats(u):
                w = u + 3
                if (due := loaded.at(u, "batch")) is not None:
                    dve.wait_ge(loaded.sem, due)
                if (due := normed.at(u - 2, 1)) is not None:
                    dve.wait_ge(normed.sem, due)
                for c in range(2):
                    dve.bn_stats(ln[:, c, 0:6], xin[:, w.parity, c, :]).then_inc(stats.sem, 1)
                    if (due := stats.at(u, f"s{c}")) is not None:
                        dve.wait_ge(stats.sem, due)
                        apart(dve, u)
                    dve.bn_aggr(ln[:, c, 6:8], ln[:, c, 0:6]).then_inc(stats.sem, 1)

            def norm2_stats(u):
                v = u - 1
                if (due := post.at(u, "x1")) is not None:
                    dve.wait_ge(post.sem, due)
                if (due := normed2.at(u - 1, 1)) is not None:
                    dve.wait_ge(normed2.sem, due)
                dve.bn_stats(l2[:, 0:6], x1[:, v.half, :]).then_inc(stats2.sem, 1)
                if (due := stats2.at(u, "s")) is not None:
                    dve.wait_ge(stats2.sem, due)
                    apart(dve, u)
                dve.bn_aggr(l2[:, 6:8], l2[:, 0:6]).then_inc(stats2.sem, 1)

            def reciprocals(u):
                if (due := den_in.at(u, "d")) is not None:
                    dve.wait_ge(den_in.sem, due)
                dve.reciprocal(rec[:, 0, :], den[:, :]).then_inc(rec_made.sem, 1)
                if (due := rec_made.at(u, "r")) is not None:
                    dve.wait_ge(rec_made.sem, due)
                if (due := rec_kept.at(u - 1, "k")) is not None:
                    dve.wait_ge(rec_kept.sem, due)
                dve.tensor_tensor(rec[:, 1, :], rec[:, 0, :], mden[:, :], ALU.mult
                                  ).then_inc(rec_made.sem, 1)

            def tile_of(u, name):
                if (due := ready.at(u, name)) is not None:
                    dve.wait_ge(ready.sem, due)
                return tiles[ready.slot(u, name, NSLOT)]


            def split_maxima(u, step):
                if not (u + 1).has():
                    return
                if step == 0:
                    if (due := drained.at(u, ("max", 31))) is not None:
                        dve.wait_ge(drained.sem, due)
                    dve.tensor_scalar(mxr[:, 0, :], mx[:, :], -1.0, None, ALU.mult).then_inc(maxsplit.sem, 1)
                if step == 1:
                    dve.wait_ge(maxsplit.sem, maxsplit.at(u, "neg"))
                    dve.tensor_copy(mxp[:, 0, :], mxr[:, 0, :]).then_inc(maxsplit.sem, 1)
                if step == 2:
                    dve.wait_ge(maxsplit.sem, maxsplit.at(u, "p0"))
                    dve.tensor_tensor(mxr[:, 1, :], mxr[:, 0, :], mxp[:, 0, :], ALU.subtract
                                      ).then_inc(maxsplit.sem, 1)
                if step == 3:
                    dve.wait_ge(maxsplit.sem, maxsplit.at(u, "r1"))
                    dve.tensor_copy(mxp[:, 1, :], mxr[:, 1, :]).then_inc(maxsplit.sem, 1)
                if step == 4:
                    dve.wait_ge(maxsplit.sem, maxsplit.at(u, "p1"))
                    dve.tensor_tensor(mxp[:, 2, :], mxr[:, 1, :], mxp[:, 1, :], ALU.subtract
                                      ).then_inc(maxsplit.sem, 1)

            def choose(u, step):
                if not (u - 2).has():
                    return
                if step == 0:
                    dve.tensor_copy(lg[:, :], tile_of(u, "logits")[:, 0:E]).then_inc(drained.sem, 1)
                if step == 1:
                    if (due := drained.at(u, "logits")) is not None:
                        dve.wait_ge(drained.sem, due)
                        apart(dve, u)
                    dve.max(v8[:, :], lg[:, :]).then_inc(choice.sem, 1)
                if step == 2:
                    if (due := choice.at(u, "v8")) is not None:
                        dve.wait_ge(choice.sem, due)
                        apart(dve, u)
                    dve.max_index(i8[:, :], v8[:, :], lg[:, :]).then_inc(choice.sem, 1)
                if step == 3:
                    if (due := choice.at(u, "i8")) is not None:
                        dve.wait_ge(choice.sem, due)
                    dve.tensor_copy(i8f[:, :], i8[:, :]).then_inc(choice.sem, 1)
                if step == 4:
                    if (due := choice.at(u, "i8f")) is not None:
                        dve.wait_ge(choice.sem, due)
                    for j in range(2):
                        dve.tensor_scalar(sel[:, j, :], io[:, 8:16], i8f[:, j:j + 1], None, ALU.is_equal
                                          ).then_inc(choice.sem, 1)
                if step == 5:
                    if (due := choice.at(u, "s1")) is not None:
                        dve.wait_ge(choice.sem, due)
                    dve.tensor_tensor(selb[:, :], sel[:, 0, :], sel[:, 1, :], ALU.add).then_inc(choice.sem, 1)
                    if (due := gate_exp.at(u - 1, "e")) is not None:
                        dve.wait_ge(gate_exp.sem, due)
                    dve.tensor_tensor(gap[:, :], v8[:, 1:2], v8[:, 0:1], ALU.subtract).then_inc(choice.sem, 1)

            def weigh(u, step):
                v = u - 2
                if not v.has():
                    return
                if step == 0:
                    if (due := gate_exp.at(u, "e")) is not None:
                        dve.wait_ge(gate_exp.sem, due)
                    dve.tensor_scalar(ex1[:, :], ex[:, :], 1.0, None, ALU.add).then_inc(weight.sem, 1)
                if step == 1:
                    if (due := weight.at(u, "ex1")) is not None:
                        dve.wait_ge(weight.sem, due)
                    dve.reciprocal(xa[:, v.half, 0, T:T + 1], ex1[:, :]).then_inc(weight.sem, 1)
                if step == 2:
                    if (due := weight.at(u, "w0")) is not None:
                        dve.wait_ge(weight.sem, due)
                    dve.tensor_tensor(xa[:, v.half, 1, T:T + 1], xa[:, v.half, 0, T:T + 1], ex[:, :],
                                      ALU.mult).then_inc(weight.sem, 1)
                    for j in range(2):
                        dve.tensor_copy(xa[:, v.half, j, T + 1:T + 2], tok[:, :]).then_inc(weight.sem, 1)
                if step == 3:
                    if (due := weight.at(u, "t1")) is not None:
                        dve.wait_ge(weight.sem, due)
                    dve.tensor_scalar(tok[:, :], tok[:, :], float(P), None, ALU.add).then_inc(weight.sem, 1)

            def rows_of(u, step):
                v = u - 2
                if not v.has():
                    return
                if step == 0:
                    t = tile_of(u, "ranks")
                    dve.tensor_tensor(rk[:, 0, :], t[:, 0:E], counts[:, :], ALU.add).then_inc(place.sem, 1)
                    if (due := place.at(u, "rk1")) is not None:
                        dve.wait_ge(place.sem, due)
                    dve.tensor_tensor(counts[:, :], t[:, E:2 * E], counts[:, :], ALU.add
                                      ).then_inc(drained.sem, 1)
                    dve.tensor_tensor(rk[:, 1, :], rk[:, 0, :], io[:, 16:24], ALU.add).then_inc(place.sem, 1)
                if step == 1:
                    if (due := place.at(u, "rk2")) is not None:
                        dve.wait_ge(place.sem, due)
                    for j in range(2):
                        dve.scalar_tensor_tensor(out=junk[:, j, :], in0=sel[:, j, :], scalar=1.0,
                                                 in1=rk[:, 1, :], op0=ALU.mult, op1=ALU.mult,
                                                 accum_out=posf[:, j:j + 1]).then_inc(place.sem, 1)
                if step == 2:
                    if (due := place.at(u, "p1")) is not None:
                        dve.wait_ge(place.sem, due)
                    if (due := routed.at(u - 2, 1)) is not None:
                        dve.wait_ge(routed.sem, due)
                    dve.tensor_copy(pos[:, v.half, :], posf[:, :]).then_inc(place.sem, 1)

            def maxima_out(u):
                t = tile_of(u, "maxT")
                if (due := maxrows.at(u - 1, "m")) is not None:
                    dve.wait_ge(maxrows.sem, due)
                dve.tensor_copy(mxt[:, :], t[:, :].bitcast(BF16)[0:96, 0:P]).then_inc(drained.sem, 1)

            def projection_out(u, side):
                w = u + 3
                t = tile_of(u, "qk"[side])
                dve.wait_ge(loaded.sem, loaded.at(u if u.half == 1 else u - 1, "batch"))
                if (due := split.at(u - 1, (side, 1))) is not None:
                    dve.wait_ge(split.sem, due)
                dve.scalar_tensor_tensor(
                    out=qkf[:, w.half, side, :], in0=t[:, :],
                    scalar=bqk[:, side, w.half:w.half + 1], in1=mb[:, w.parity, :],
                    op0=ALU.add, op1=ALU.mult).then_inc(drained.sem, 1)

            def maximum(u, j):
                if not (u + 1).has():
                    return
                if j == 0 and (due := maxsplit.at(u - 1, "neg")) is not None:
                    dve.wait_ge(maxsplit.sem, due)
                t = tile_of(u, ("max", j))
                dve.tensor_reduce(mx[:, j:j + 1], t[:, :], X, ALU.max).then_inc(drained.sem, 1)

            def unit(u):
                m = 0
                for s, n in enumerate(MAX_SHARE):
                    for j in range(n):
                        maximum(u, m + j)
                        if s == 4:
                            choose(u, j + 1)
                    m += n
                    if s == 1 and (u - 2).has():
                        dve.tensor_copy(xt[:, :, :], tile_of(u, "xT")[:, :].rearrange("p (c o) -> p c o", c=4)
                                        ).then_inc(drained.sem, 1)
                    if s == 2 and (u - 1).has():
                        reciprocals(u)
                    if s == 3:
                        choose(u, 0)
                    if s == 3 and (u + 3).has() and u.half == 1:
                        norm_stats(u)
                    if s == 5:
                        rows_of(u, 0)
                    if s == 6:
                        split_maxima(u, 0)
                        rows_of(u, 1)
                        split_maxima(u, 1)
                        weigh(u, 0)
                        split_maxima(u, 2)
                        rows_of(u, 2)
                        split_maxima(u, 3)
                        weigh(u, 1)
                        split_maxima(u, 4)
                        weigh(u, 2)
                    if s == 6 and (u - 1).has():
                        norm2_stats(u)
                    if s == 6:
                        weigh(u, 3)
                    if s == 6 and (u + 3).has():
                        projection_out(u, 0)
                    if s == 7 and (u + 1).has():
                        maxima_out(u)
                    if s == 7 and (u + 3).has():
                        projection_out(u, 1)
                if (u + 1).has():
                    w = u + 1
                    t = tile_of(u, "v")
                    dve.tensor_tensor(vt[:, :, :], t[:, :].rearrange("p (c o) -> p c o", c=4),
                                      bv_s[:, w.half * P:w.half * P + P].rearrange("p (a o) -> p a o", a=1)
                                      .broadcast_to([P, 4, P]), ALU.add).then_inc(drained.sem, 1)
                    if (due := drained.at(u, "v")) is not None:
                        dve.wait_ge(drained.sem, due)
                    if (due := pved.at(u - 1, 7)) is not None:
                        dve.wait_ge(pved.sem, due)
                    dve.tensor_tensor(vp[w.half][:, :, :, 0:D],
                                      vt[:, :, :].rearrange("p c (h d) -> p c h d", d=D),
                                      mc[:, w.parity, :].rearrange("p (c a b) -> p c a b", a=1, b=1)
                                      .broadcast_to([P, 4, UH, D]), ALU.mult).then_inc(vmade.sem, 1)


            def plan_tiles():
                at_ = [0]

                def do(ins):
                    at_[0] += 1
                    ins.then_inc(plan, 1)
                    dve.wait_ge(plan, at_[0])

                NTF, CUM, SEG, T0, T1 = range(5)
                do(dve.tensor_tensor(f[:, T0, :], counts[:, :], io[:, 16:24], ALU.add))
                do(dve.tensor_copy(padrow[:, :], f[0:1, T0, :]))
                do(dve.tensor_scalar(f[:, T1, :], counts[:, :], float(P - 1), None, ALU.add))
                do(dve.tensor_copy(fi[:, 0, :], f[:, T1, :]))
                do(dve.tensor_scalar(fi[:, 1, :], fi[:, 0, :], 7, None, ALU.arith_shift_right))
                do(dve.tensor_copy(f[:, NTF, :], fi[:, 1, :]))
                do(dve.tensor_copy(f[:, CUM, 0:1], f[:, NTF, 0:1]))
                for e in range(1, E):
                    do(dve.tensor_tensor(f[:, CUM, e:e + 1], f[:, CUM, e - 1:e], f[:, NTF, e:e + 1], ALU.add))
                do(dve.tensor_scalar(f[:, SEG, :], f[:, NTF, :], -float(P), float(CAP), ALU.mult, ALU.add))
                nt_e = [1, NT, E]
                num_n = io[0:1, 32:32 + NT].rearrange("p (n o) -> p n o", o=1).broadcast_to(nt_e)
                g0 = ge[:, 0, :].rearrange("p (n e) -> p n e", e=E)
                g1 = ge[:, 1, :].rearrange("p (n e) -> p n e", e=E)
                g2 = ge[:, 2, :].rearrange("p (n e) -> p n e", e=E)
                do(dve.tensor_copy(g2, num_n))
                do(dve.tensor_tensor(g0, g2, f[0:1, CUM:CUM + 1, :].broadcast_to(nt_e), ALU.is_ge))
                do(dve.tensor_tensor(g1, g0, f[0:1, SEG:SEG + 1, :].broadcast_to(nt_e), ALU.mult))
                do(dve.tensor_reduce(tf[:, 0, :], g0, X, ALU.add))
                do(dve.tensor_reduce(tf[:, 1, :], g1, X, ALU.add))
                do(dve.tensor_scalar(tf[:, 2, :], tf[:, 0, :], float(E - 1), None, ALU.min))
                do(dve.tensor_copy(ends[:, :], f[0:1, CUM, :]))
                do(dve.tensor_scalar(tf[:, 4, :], tf[:, 2, :], float(WRING), float(-WRING), ALU.is_ge, ALU.mult))
                do(dve.tensor_scalar(tf[:, 5, :], tf[:, 2, :], float(2 * WRING), float(-WRING), ALU.is_ge, ALU.mult))
                do(dve.tensor_tensor(tf[:, 6, :], tf[:, 4, :], tf[:, 5, :], ALU.add))
                do(dve.tensor_tensor(tf[:, 7, :], tf[:, 6, :], tf[:, 2, :], ALU.add))
                do(dve.tensor_scalar(tab[:, OFFSET, :], tf[:, 7, :], float(WN), None, ALU.mult))
                do(dve.tensor_copy(tab[:, EXPERT, :], tf[:, 2, :]))
                do(dve.tensor_scalar(tf[:, 3, :], io[0:1, 32:32 + NT], float(P), None, ALU.mult))
                do(dve.tensor_tensor(tab[:, ROWS, :], tf[:, 3, :], tf[:, 1, :], ALU.add))
                do(dve.tensor_scalar(pairf[:, 0:1], f[0:1, CUM, E - 1:E], 1.0, None, ALU.add))
                do(dve.tensor_copy(pairi[:, 0:1], pairf[:, 0:1]))
                do(dve.tensor_scalar(pairi[:, 1:2], pairi[:, 0:1], 1, None, ALU.arith_shift_right))
                do(dve.tensor_scalar(pairi[:, 2:3], pairi[:, 1:2], 2.0, None, ALU.mult))
                do(dve.tensor_scalar(pairi[:, 3:4], pairi[:, 2:3], 1.0, None, ALU.subtract))

            iterations(dve, unit)
            dve.wait_ge(drained.sem, drained.total())
            plan_tiles()

        @block.tensor
        def _(pe):
            pe.wait_ge(const_made, MADE)
            pe.wait_ge(ones_made, 4)

            def slot(u, name):
                if (due := drained.at(u, name, back=NSLOT)) is not None:
                    pe.wait_ge(drained.sem, due)
                return tiles[ready.slot(u, name, NSLOT)]

            def scores(u, s, j):
                g, c = s // 4, s % 4
                if s == 0 and j == 0:
                    if (due := maxrows.at(u - 1, "m")) is not None:
                        pe.wait_ge(maxrows.sem, due)
                if (due := exped.at(u, (s, j), back=2)) is not None:
                    pe.wait_ge(exped.sem, due)
                for i in range(2):
                    h = 4 * g + 2 * j + i
                    last = nc.tensor.matmul(sc[j][:, i, :],
                                            ks[u.half][0:ALL_ROWS, h, c * P:c * P + P],
                                            qs[u.half][0:ALL_ROWS, h, :], start=True, stop=True)
                last.then_inc(scored.sem, 1)

            def raw_scores(u, m):
                w, h, c = u + 1, m // 4, m % 4
                if m % 16 == 0:
                    if (due := stacked[m // 16].at(u - 1, "g")) is not None:
                        pe.wait_ge(stacked[m // 16].sem, due)
                t = slot(u, ("max", m))
                nc.tensor.matmul(t[:, :], qs[w.half][0:RAW_ROWS, h, c * P:c * P + P],
                                 ks[w.half][0:RAW_ROWS, h, :], start=True, stop=True
                                 ).then_inc(ready.sem, 1)

            def product(u, s, pair):
                g, c = s // 4, s % 4
                if pair == 0:
                    if s == 0:
                        if (due := vmade.at(u - 1, "v")) is not None:
                            pe.wait_ge(vmade.sem, due)
                        if (due := pv_out.at(u - 1, 1)) is not None:
                            pe.wait_ge(pv_out.sem, due)
                    if s == 4:
                        pe.wait_ge(pv_out.sem, pv_out.at(u, 0))
                    pe.wait_ge(exped.sem, exped.at(u, (s, 1)))
                for i in (2 * pair, 2 * pair + 1):
                    last = nc.tensor.matmul(pvb[32 * i:32 * i + 32, :], vp[u.half][:, c, 4 * g + i, :],
                                            pr[s % 2][:, i, :], start=(c == 0), stop=(c == 3))
                if pair:
                    last.then_inc(pved.sem, 1)

            def project(u, side):
                w = u + 3
                at = u if u.half == 1 else u - 1
                t = slot(u, "qk"[side])
                if side == 0:
                    pe.wait_ge(normed.sem, normed.at(at, 1))
                else:
                    pe.wait_ge(loaded.sem, loaded.at(at, "batch"))
                weight, source = ((wq_s, xh), (wk_s, cin))[side]
                for c in range(2):
                    last = nc.tensor.matmul(t[:, :], weight[:, c, w.half * P:w.half * P + P],
                                            source[:, w.parity, c, :], start=(c == 0), stop=(c == 1))
                last.then_inc(ready.sem, 1)

            def values(u):
                w = u + 1
                t = slot(u, "v")
                for s in range(4):
                    for c in range(2):
                        last = nc.tensor.matmul(t[:, s * P:s * P + P],
                                                cin[:, w.parity, c, s * P:s * P + P],
                                                wv_s[:, c, w.half * P:w.half * P + P],
                                                start=(c == 0), stop=(c == 1))
                last.then_inc(ready.sem, 1)

            def unit(u):
                m = 0
                for s, n in enumerate(MAX_SHARE):
                    todo = list(range(m, m + n)) if (u + 1).has() else []
                    m += n

                    def raw(count):
                        for _ in range(min(count, len(todo))):
                            raw_scores(u, todo.pop(0))

                    if u.has():
                        scores(u, s, 0)
                    raw(2)
                    if u.has():
                        scores(u, s, 1)
                    raw(2)
                    if u.has() and s:
                        product(u, s - 1, 0)
                    raw(1)
                    if u.has() and s:
                        product(u, s - 1, 1)
                    raw(n)
                    if s == 1 and (u - 2).has():
                        pe.wait_ge(normed2.sem, normed2.at(u - 1, 0))
                        t = slot(u, "xT")
                        for c in range(4):
                            last = nc.tensor.transpose(t[:, c * P:c * P + P],
                                                       xa[:, u.half, 0, c * P:c * P + P], idf[:, :])
                        last.then_inc(ready.sem, 1)
                    if s == 3 and (u - 2).has():
                        pe.wait_ge(drained.sem, drained.at(u, "xT"))
                        t = slot(u, "logits")
                        for c in range(4):
                            last = nc.tensor.matmul(t[:, 0:E], xt[:, c, :], gate_s[:, c, :],
                                                    start=(c == 0), stop=(c == 3))
                        last.then_inc(ready.sem, 1)
                    if s == 5 and (u - 2).has():
                        pe.wait_ge(choice.sem, choice.at(u, "selb"))
                        t = slot(u, "ranks")
                        nc.tensor.matmul(t[:, 0:E], upper[:, :], selb[:, :], start=True, stop=True)
                        nc.tensor.matmul(t[:, E:2 * E], ones[:, :], selb[:, :], start=True, stop=True
                                         ).then_inc(ready.sem, 1)
                    if s == 6 and (u + 3).has():
                        project(u, 0)
                    if s == 7 and (u + 1).has():
                        pe.wait_ge(maxsplit.sem, maxsplit.at(u, "p2"))
                        t = slot(u, "maxT")
                        nc.tensor.transpose(t[:, :].bitcast(BF16)[0:96, 0:P],
                                            mxp[:, :, :].rearrange("p i m -> p (i m)"), idb[:, :]
                                            ).then_inc(ready.sem, 1)
                    if s == 7 and (u + 3).has():
                        project(u, 1)
                if u.has():
                    product(u, 7, 0)
                    product(u, 7, 1)
                if (u + 1).has():
                    values(u)

            iterations(pe, unit)


def experts(nc, load_expert, wring, weights_in, out, routed_d, idf, tab, ends, pairi):
    st = ExitStack()
    with st:
        def sb(name, shape, dt=F32):
            return st.enter_context(nc.sbuf_tensor(name, shape, dt))

        def sem(name):
            return st.enter_context(nc.semaphore(name))

        xl = sb("xl", [P, 2, ROW])
        xt = [sb(f"xtile{i}", [P, 4, P]) for i in range(2)]
        sg = sb("sg", [P, 2, I])
        ac = sb("ac", [P, 2, I])
        at = sb("at", [P, len(ICHUNKS), P])
        y = sb("y", [P, 2, T])
        meta = sb("meta", [P, 2, 2])
        metay = sb("metay", [P, 2, 1])
        ids = sb("ids", [P, 2, 1], U32)

        def pb(name):
            return st.enter_context(nc.psum_tensor(name, [P, T], F32))

        xtp, atp, dp = pb("xtp"), pb("atp"), pb("dp")
        gp = [pb(f"gp{i}") for i in range(2)]
        up = [pb(f"up{i}") for i in range(2)]

        passed = sem("passed")
        experts_in = sem("experts_in")
        xl_in = [sem(f"xl_in{k}") for k in range(2)]
        xt_ready, xt_made = sem("xt_ready"), sem("xt_made")
        copied = sem("copied")
        up_done, silu_done, act_done = sem("up_done"), sem("silu_done"), sem("act_done")
        at_ready, at_made = sem("at_ready"), sem("at_made")
        down_done, y_made, y_added, noted = sem("down_done"), sem("y_made"), sem("y_added"), sem("noted")
        block = st.enter_context(nc.Block())

        def entry(eng, row, n, top):
            return eng.value_load(tab[0:1, row, bass.ds(n, 1)], min_val=0, max_val=top)

        def pairs(eng):
            return eng.value_load(pairi[0:1, 1:2], min_val=TOKENS // P,
                                  max_val=(2 * TOKENS // P + E) // 2)

        def last_tile(eng):
            return eng.value_load(pairi[0:1, 3:4], min_val=2 * TOKENS // P - 1, max_val=NT - 1)

        def tiles(eng, tile, count):
            tile(0, 0)
            tile(1, 1)
            with eng.Fori(1, count) as i:
                tile(i * 2, 0)
                tile(i * 2 + 1, 1)

        def later(n, back):
            return not isinstance(n, int) or n >= back

        @block.sync
        def _(sp):
            for e in range(WRING):
                sp.wait_ge(weights_in[e], 48)
                sp.sem_inc(experts_in, 1)
            for e in range(WRING, E):
                ended = sp.value_load(ends[0:1, e - WRING:e - WRING + 1], min_val=0, max_val=NT)
                sp.wait_ge(down_done, ended + 1)
                load_expert(sp, e)
                sp.wait_ge(weights_in[e], 48)
                sp.sem_inc(experts_in, 1)

        @block.vector
        def _(dve):
            count = pairs(dve)

            def fetch(n, k):
                dve.wait_ge(xt_ready, n + 1)
                if later(n, 2):
                    dve.wait_ge(up_done, n - 1)
                dve.tensor_copy(xt[k][:, :, :], xtp[:, :].rearrange("p (c o) -> p c o", c=4)
                                ).then_inc(copied, 1)
                dve.tensor_copy(meta[:, k, :], xl[:, k, T:T + 2]).then_inc(xt_made, 1)

            def note(n, k):
                if later(n, 2):
                    dve.wait_ge(y_added, (n - 1) * 16)
                dve.wait_ge(xt_made, n + 1)
                dve.tensor_copy(metay[:, k, :], meta[:, k, 0:1]).then_inc(noted, 1)
                dve.tensor_copy(ids[:, k, :], meta[:, k, 1:2]).then_inc(noted, 1)

            def finish(n, k):
                dve.wait_ge(at_ready, n + 1)
                if later(n, 1):
                    dve.wait_ge(down_done, n + 1)
                dve.tensor_copy(at[:, 0:2, :], atp[:, 0:2 * P].rearrange("p (c o) -> p c o", c=2)
                                ).then_inc(copied, 1)
                dve.tensor_copy(at[0:I - 2 * P, 2, :], atp[0:I - 2 * P, 2 * P:3 * P]
                                ).then_inc(at_made, 1)

            def scale(n, k):
                dve.wait_ge(down_done, n + 2)
                dve.wait_ge(noted, (n + 1) * 2)
                dve.tensor_scalar(y[:, k, :], dp[:, :], metay[:, k, 0:1], None, ALU.mult
                                  ).then_inc(y_made, 1)

            def tile(n, k):
                prev = not (isinstance(n, int) and n == 0)
                if prev:
                    finish(n - 1, 1 - k)
                fetch(n + 1, 1 - k)
                if prev:
                    scale(n - 1, 1 - k)
                note(n, k)
                dve.wait_ge(silu_done, n + 1)
                if later(n, 2):
                    dve.wait_ge(at_ready, n - 1)
                dve.tensor_tensor(ac[:, k, :], sg[:, k, :], up[k][:, 0:I], ALU.mult).then_inc(act_done, 1)

            fetch(0, 0)
            tiles(dve, tile, count)
            last = last_tile(dve)
            finish(last, 1)
            scale(last, 1)

        @block.scalar
        def _(act):
            count = pairs(act)
            def load(n, k):
                if later(n, 2):
                    act.wait_ge(xt_made, n - 1)
                row = entry(act, ROWS, n, E * CAP + 3 * P)
                act.dma_start(xl[:, k, :], routed_d[bass.ds(row, P), :]).then_inc(xl_in[k], 16)

            def tile(n, k):
                load(n + 2, k)
                act.wait_ge(up_done, n + 1)
                if later(n, 2):
                    act.wait_ge(act_done, n - 1)
                nc.scalar.activation(sg[:, k, :], gp[k][:, 0:I], ACT.Silu).then_inc(silu_done, 1)

            load(0, 0)
            load(1, 1)
            tiles(act, tile, count)
            for k in range(2):
                act.wait_ge(xl_in[k], (count + 1) * 16)
            act.sem_inc(passed, 1)

        @block.gpsimd
        def _(pool):
            count = pairs(pool)

            def tile(n, k):
                pool.wait_ge(y_made, n + 1)
                pool.wait_ge(noted, (n + 1) * 2)
                if later(n, 1):
                    pool.wait_ge(y_added, n * 16)
                pool.sem_inc(passed, 1)
                pool.indirect_dma_start(out, bass.IndirectOffsetOnAxis(ap=ids[:, k, :], axis=0),
                                        y[:, k, :], None, compute_op=ALU.add).then_inc(y_added, 16)

            tiles(pool, tile, count)
            pool.wait_ge(y_added, count * 32)

        @block.tensor
        def _(pe):
            count = pairs(pe)

            def transpose_rows(n, k):
                pe.wait_ge(xl_in[k], ((n - k) // 2 + 1) * 16)
                if later(n, 1):
                    pe.wait_ge(xt_made, n)
                for c in range(4):
                    last = nc.tensor.transpose(xtp[:, c * P:c * P + P], xl[:, k, c * P:c * P + P], idf[:, :])
                last.then_inc(xt_ready, 1)

            def gate_up(n, k):
                expert = entry(pe, EXPERT, n, E - 1)
                off = entry(pe, OFFSET, n, (WRING - 1) * WN)
                pe.wait_ge(experts_in, expert + 1)
                pe.wait_ge(xt_made, n + 1)
                if later(n, 2):
                    pe.wait_ge(act_done, n - 1)
                for dst, o in ((gp[k], 0), (up[k], I)):
                    for c in range(4):
                        last = nc.tensor.matmul(dst[:, 0:I], xt[k][:, c, :],
                                                wring[:, bass.ds(off + (c * 2 * I + o), I)],
                                                start=(c == 0), stop=(c == 3))
                last.then_inc(up_done, 1)

            def transpose_act(n, k):
                pe.wait_ge(act_done, n + 1)
                if later(n, 1):
                    pe.wait_ge(at_made, n)
                for c, (o, w) in enumerate(ICHUNKS):
                    last = nc.tensor.transpose(atp[0:w, c * P:c * P + P], ac[:, k, o:o + w], idf[:, :])
                last.then_inc(at_ready, 1)

            def down(n, k):
                off = entry(pe, OFFSET, n, (WRING - 1) * WN)
                pe.wait_ge(at_made, n + 1)
                if later(n, 1):
                    pe.wait_ge(y_made, n)
                for c, (o, w) in enumerate(ICHUNKS):
                    last = nc.tensor.matmul(dp[:, :], at[0:w, c, :], wring[0:w, bass.ds(off + (W1N + c * T), T)],
                                            start=(c == 0), stop=(c == len(ICHUNKS) - 1))
                last.then_inc(down_done, 1)

            def tile(n, k):
                prev = not (isinstance(n, int) and n == 0)
                gate_up(n, k)
                if prev:
                    transpose_act(n - 1, 1 - k)
                transpose_rows(n + 1, 1 - k)
                if prev:
                    down(n - 1, 1 - k)

            pe.sem_inc(down_done, 1)
            transpose_rows(0, 0)
            tiles(pe, tile, count)
            last = last_tile(pe)
            transpose_act(last, 1)
            down(last, 1)


def kernel(**inputs):
    import concourse.bacc as bacc
    from concourse.bass_utils import run_bass_kernel_spmd

    def f32(name):
        return np.asarray(inputs[name])

    iotas = np.zeros((P, 96), np.float32)
    iotas[:, 0] = np.arange(P)
    iotas[:, 1] = -0.5
    iotas[:, 8:16] = np.arange(E)
    iotas[:, 16:24] = np.arange(E) * CAP
    iotas[:, 32:32 + NT] = np.arange(NT)
    arrays = {
        "x": f32("x").reshape(TOKENS, T),
        "ctxt": f32("ctx_2048").reshape(TOKENS, T),
        "mask": f32("mask_Bx1x2048_fk1").reshape(B, T),
        "wq": f32("L0_xattn_Wq").T, "wk": f32("L0_xattn_Wk").T, "wv": f32("L0_xattn_Wv").T,
        "maskc": f32("mask_Bx1x2048_fk1").reshape(B, 4, P).transpose(2, 0, 1),
        "bq": f32("L0_xattn_bq").reshape(2, P).T, "bk": f32("L0_xattn_bk").reshape(2, P).T, "bv": f32("L0_xattn_bv"),
        "gate": f32("L0_ffn_gate_w").T,
        "w1": f32("L0_ffn_w1").transpose(0, 2, 1), "w2": f32("L0_ffn_w2").transpose(0, 2, 1),
        "ident": np.eye(P, dtype=np.float32),
        "ut": np.triu(np.ones((P, P), np.float32), 1),
        "iotas": iotas,
    }
    arrays = {k: np.ascontiguousarray(v) for k, v in arrays.items()}
    nc = bacc.Bacc("TRN2", target_bir_lowering=False, num_devices=1)
    args = {k: nc.dram_tensor(k + "_dram", v.shape, mybir.dt.from_np(v.dtype), kind="ExternalInput").ap()
            for k, v in arrays.items()}
    out = nc.dram_tensor("out_dram", (TOKENS + P, T), F32, kind="ExternalOutput").ap()
    build(nc, out=out, **args)
    r = run_bass_kernel_spmd(nc, [{k + "_dram": v for k, v in arrays.items()}], core_ids=[0])
    return r.results[0]["out_dram"][:TOKENS].reshape(B, C, T)
```
